# Optimizing a Trainium2 kernel written in Bass

```python
import numpy as np
import jax
import jax.numpy as jnp

def _softmax(x, axis=-1):
    return jax.nn.softmax(x, axis=axis)

def _gelu(x):
    return jax.nn.gelu(x, approximate=True)

def _silu(x):
    return jax.nn.silu(x)

def _sigmoid(x):
    return jax.nn.sigmoid(x)

def _layernorm(x, axis=-1, eps=1e-05):
    m = jnp.mean(x, axis=axis, keepdims=True)
    v = jnp.var(x, axis=axis, keepdims=True)
    return (x - m) / jnp.sqrt(v + eps)

def _scatter_add(tgt, idx, src, axis=0):
    return tgt.at[idx].add(src)

def _segment_sum(src, seg, n):
    return jax.ops.segment_sum(src, seg, n)
kernel_name = 'mk_seq_preln_d1_jaxref_r2_7df2fe'

def setup_inputs(seed: int=0):
    np.random.seed(seed)
    _w = jnp.asarray

    def _L0_attn_setup():
        import jax, jax.numpy as jnp
        import numpy as np
        from jax import lax
        N_EMBD = 512
        N_HEAD = 16
        HEAD_DIM = N_EMBD // N_HEAD
        EPS = 1e-06
        B, T = (4, 1024)

        def _feature_map(x):
            return jax.nn.elu(x) + 1.0
        key = jax.random.key(seed)
        ks = jax.random.split(key, 5)
        scale = 1.0 / np.sqrt(N_EMBD)
        return {'x': jax.random.normal(ks[0], (B, T, N_EMBD), jnp.float32), 'W_attn': jax.random.normal(ks[1], (N_EMBD, 3 * N_EMBD), jnp.float32) * scale, 'b_attn': jax.random.normal(ks[2], (3 * N_EMBD,), jnp.float32) * 0.01, 'W_proj': jax.random.normal(ks[3], (N_EMBD, N_EMBD), jnp.float32) * scale, 'b_proj': jax.random.normal(ks[4], (N_EMBD,), jnp.float32) * 0.01}
    _L0_attn_in = _L0_attn_setup()

    def _L0_ffn_setup():
        import jax, jax.numpy as jnp
        import numpy as np
        FP8_MAX = 448.0
        SCALE = 1.0
        _FP8_DTYPE = getattr(jnp, 'float8_e4m3fn', jnp.float16)

        def quantize_e4m3(t, scale):
            return jnp.clip(t / scale, -FP8_MAX, FP8_MAX).astype(_FP8_DTYPE)
        key = jax.random.key(seed)
        kx, kw = jax.random.split(key)
        B, N, C, F = (8, 2048, 512, 512)
        x = jax.random.normal(kx, (B, N, C), dtype=jnp.float32)
        weight = jax.random.normal(kw, (F, C), dtype=jnp.float32) * 0.02
        bias = jnp.zeros((F,), dtype=jnp.float32)
        return {'x': x, 'weight': weight, 'bias': bias}
    _L0_ffn_in = _L0_ffn_setup()
    _d = {'L0_attn_x': _L0_attn_in['x'], 'L0_attn_W_attn': _L0_attn_in['W_attn'], 'L0_attn_b_attn': _L0_attn_in['b_attn'], 'L0_attn_W_proj': _L0_attn_in['W_proj'], 'L0_attn_b_proj': _L0_attn_in['b_proj'], 'L0_ffn_weight': _L0_ffn_in['weight'], 'L0_ffn_bias': _L0_ffn_in['bias']}
    _x0 = _d['L0_attn_x']
    _d['L0_attn_x'] = jax.random.normal(jax.random.fold_in(jax.random.key(seed), 1), (8, 1024, 512), dtype=_x0.dtype)
    del _x0
    return _d

def reference(L0_attn_x, L0_attn_W_attn, L0_attn_b_attn, L0_attn_W_proj, L0_attn_b_proj, L0_ffn_weight, L0_ffn_bias):

    def _L0_attn_ref(x, W_attn, b_attn, W_proj, b_proj):
        import jax, jax.numpy as jnp
        import numpy as np
        from jax import lax
        N_EMBD = 512
        N_HEAD = 16
        HEAD_DIM = N_EMBD // N_HEAD
        EPS = 1e-06
        B, T = (4, 1024)

        def _feature_map(x):
            return jax.nn.elu(x) + 1.0
        Bb, Tt, C = x.shape
        qkv = x @ W_attn + b_attn
        q, k, v = jnp.split(qkv, 3, axis=-1)

        def to_heads(t):
            return t.reshape(Bb, Tt, N_HEAD, HEAD_DIM).transpose(1, 0, 2, 3)
        q = _feature_map(to_heads(q))
        k = _feature_map(to_heads(k))
        v = to_heads(v)

        def step(carry, inp):
            kv, ksum = carry
            qt, kt, vt = inp
            kv = kv + kt[..., :, None] * vt[..., None, :]
            ksum = ksum + kt
            num = jnp.einsum('bhi,bhij->bhj', qt, kv)
            den = jnp.einsum('bhi,bhi->bh', qt, ksum)[..., None] + EPS
            return ((kv, ksum), num / den)
        init = (jnp.zeros((Bb, N_HEAD, HEAD_DIM, HEAD_DIM), x.dtype), jnp.zeros((Bb, N_HEAD, HEAD_DIM), x.dtype))
        _, y = lax.scan(step, init, (q, k, v))
        y = y.transpose(1, 0, 2, 3).reshape(Bb, Tt, C)
        return y @ W_proj + b_proj

    def _L0_ffn_ref(x, weight, bias):
        import jax, jax.numpy as jnp
        import numpy as np
        FP8_MAX = 448.0
        SCALE = 1.0
        _FP8_DTYPE = getattr(jnp, 'float8_e4m3fn', jnp.float16)

        def quantize_e4m3(t, scale):
            return jnp.clip(t / scale, -FP8_MAX, FP8_MAX).astype(_FP8_DTYPE)
        B, N, C = x.shape
        x2d = x.reshape(B * N, C)
        x_mat = quantize_e4m3(x2d, SCALE).astype(jnp.float16)
        w_mat = quantize_e4m3(weight, SCALE).astype(jnp.float16)
        out2d = (x_mat @ w_mat.T).astype(jnp.float32) * (SCALE * SCALE)
        out2d = out2d + bias
        return out2d.reshape(B, N, -1)
    x = L0_attn_x
    x = x + _L0_attn_ref(_layernorm(x, axis=-1), L0_attn_W_attn, L0_attn_b_attn, L0_attn_W_proj, L0_attn_b_proj)
    x = x + _L0_ffn_ref(_layernorm(x, axis=-1), L0_ffn_weight, L0_ffn_bias)
    return x

_drawn_inputs = setup_inputs


def setup_inputs(seed=0):
    import zlib

    import numpy as np

    out = dict(_drawn_inputs(seed))
    spreads = {'L0_ffn_bias': (0.0, 0.1)}
    factors = {'L0_attn_b_attn': 4.521, 'L0_attn_b_proj': 4.684}
    for name, (base, spread) in spreads.items():
        noise = np.random.default_rng([zlib.crc32(name.encode()), seed]).standard_normal(out[name].shape)
        drawn = base * np.exp(spread * noise) if base else spread * noise
        out[name] = jnp.asarray(drawn.astype(out[name].dtype))
    for name, factor in factors.items():
        out[name] = (out[name] * factor).astype(out[name].dtype)
    return out
```

```python
from contextlib import ExitStack

import concourse.bass as bass
from concourse import mybir

ALU = mybir.AluOpType
ACT = mybir.ActivationFunctionType
AX = mybir.AxisListType
F32 = mybir.dt.float32
F32R = mybir.dt.float32r
F16 = mybir.dt.float16
BF16 = mybir.dt.bfloat16
F8 = mybir.dt.float8e4
I32 = mybir.dt.int32

D = 512
B = 8
T = 1024
P = 128
NT = B * T // P
NB = NT // 4
PER = T // P
LN_EPS = 1e-5
DEN_EPS = 1e-6
NX = 16
NR = 3


class Queues:

    ENGINES = ("pe", "act", "dve", "pool", "sp")

    def __init__(self):
        self.ops = {e: [] for e in self.ENGINES}
        self.count = {e: 0 for e in self.ENGINES}

    def do(self, eng, fn, *waits, tick=True):
        self.ops[eng].append((waits, fn, tick and (eng, 1)))
        if tick:
            self.count[eng] += 1
            return eng, self.count[eng]
        return None

    def dma(self, eng, fn, name, value, *waits):
        self.ops[eng].append((waits, fn, (name, 16)))
        return name, value

    def run(self, eng, e, sems):
        seen = {}
        for waits, fn, tick in self.ops[eng]:
            for name, value in waits:
                if seen.get(name, 0) < value:
                    e.wait_ge(sems[name], value)
                    seen[name] = value
            ins = fn(e)
            if tick:
                ins.then_inc(sems[tick[0]], tick[1])


def build(nc, x_d, wa_d, ba_d, wp_d, bp_d, wf_d, bf_d, out_d):
    ctx = ExitStack()
    with ctx:
        def sb(name, shape, dt):
            return ctx.enter_context(nc.sbuf_tensor(name, shape, dt))

        def psum(name):
            return ctx.enter_context(nc.psum_tensor(name, [P, 512], F32))

        xs = sb("xs", [P, NX, D], F32)
        xn = sb("xn", [P, 4, D], F32)
        xth = sb("xth", [P, 4, D], F16)
        xtl = sb("xtl", [P, 4, D], F16)
        qkv = [sb(f"qkv{i}", [P, 12, D], F32) for i in range(2)]
        ktok = sb("ktok", [P, 2, D], F32)
        rel = sb("rel", [P, 2, D], F32)
        sm = sb("sm", [P, 4, D], F32)
        state = sb("state", [P, 2, D], F32)
        delta = sb("delta", [P, D], F32)
        cum = sb("cum", [P, 2, D], F32)
        carry = sb("carry", [P, 4], F32)
        qc = sb("qc", [P, 4, D], F32)
        dene = sb("dene", [P, D], F32)
        rden = sb("rden", [P, 2, D], F32)
        y = sb("y", [P, D], F32)
        yh = sb("yh", [P, 2, D], F32R)
        yl = sb("yl", [P, 2, D], F32R)
        x2 = sb("x2", [P, 2, D], F32)
        x2t = sb("x2t", [P, 2, D], F8)
        o16 = sb("o16", [P, 2, D], F16)
        wh = sb("wh", [P, 4, 3 * D], F16)
        wl = sb("wl", [P, 4, 3 * D], F16)
        wph = sb("wph", [P, 4, D], F32R)
        wpl = sb("wpl", [P, 4, D], F32R)
        wft = sb("wft", [P, 4, D], BF16)
        causal = sb("causal", [P, P], BF16)
        blk = sb("blk", [P, P], F32)
        ident = sb("ident", [P, P], F32)
        bqk = sb("bqk", [P, 8], F32)
        bv = sb("bv", [P, D], F32)
        bp = sb("bp", [P, D], F32)
        bf = sb("bf", [P, D], F32)
        half = sb("half", [P, 1], F32)
        st1 = sb("st1", [P, 4, 12], F32)
        st2 = sb("st2", [P, 4, 12], F32)
        wm = sb("wm", [P, 8], F32)

        R = [psum(f"R{i}") for i in range(NR)]
        S = [psum(f"S{i}") for i in range(4)]
        Y = psum("Y")

        q = Queues()
        do = q.do
        dma_sems = ["wa", "wp", "wf", "bias"] + [f"xi{i}" for i in range(NX)] + [f"xo{i}" for i in range(NX)]
        sems = {n: ctx.enter_context(nc.semaphore(f"s_{n}")) for n in [*Queues.ENGINES, *dma_sems]}

        tok = {}
        ring = {"n": 0, "free": [()] * NR}

        def take():
            r = ring["n"] % NR
            ring["n"] += 1
            return r, ring["free"][r]

        def give(r, *tokens):
            ring["free"][r] = tokens

        def group(r, frees, mms, *waits):
            last = None
            for i, (o, a, b, start, stop) in enumerate(mms):
                last = do("pe", lambda e, o=o, a=a, b=b, s=start, t=stop: e.matmul(
                    o, a, b, start=s, stop=t, skip_group_check=True),
                    *(waits if i == 0 else ()), *(frees if i == 0 else ()), tick=i == len(mms) - 1)
            return last

        def transposes(r, frees, ins, *waits):
            last = None
            for i, a in enumerate(ins):
                last = do("pe", lambda e, a=a, i=i: e.transpose(R[r][:, i * P:(i + 1) * P], a, ident[:, :]),
                          *(waits if i == 0 else ()), *(frees if i == 0 else ()), tick=i == len(ins) - 1)
            return last

        def four(t):
            return t.rearrange("p (g m) -> p g m", g=4)

        def over(t):
            return t.unsqueeze(1).broadcast_to([P, 4, P])

        def load_x(m):
            i = m % NX
            waits = (tok["store", m - NX],) if m >= NX else ()
            tok["load", m] = q.dma("sp", lambda e: e.dma_start(xs[:, i, :], x_d[m * P:(m + 1) * P, :]),
                                   f"xi{i}", 16 * (m // NX + 1), *waits)

        raw = qkv[1][:, :, :].rearrange("p a n -> p (a n)").rearrange("p (k n) -> p k n", k=4)
        for m in range(4):
            load_x(m)
        tok["wa"] = q.dma("act", lambda e: e.dma_start(raw, wa_d.rearrange("(k p) n -> p k n", p=P)), "wa", 16)
        q.dma("act", lambda e: e.dma_start(bqk[:, :], ba_d[0:2 * D].rearrange("(i p) -> p i", p=P), allow_slow_non_contiguous=True), "bias", 16)
        q.dma("act", lambda e: e.dma_start(bv[:, :], ba_d[2 * D:3 * D].partition_broadcast(P)), "bias", 32)
        q.dma("act", lambda e: e.dma_start(bp[:, :], bp_d.partition_broadcast(P)), "bias", 48)
        tok["bias"] = q.dma("act", lambda e: e.dma_start(bf[:, :], bf_d.partition_broadcast(P)), "bias", 64)
        tok["wp"] = q.dma("act", lambda e: e.dma_start(sm[:, :, :], wp_d.rearrange("(k p) n -> p k n", p=P)),
                          "wp", 16)
        tok["wf"] = q.dma("act", lambda e: e.dma_start(qc[:, :, :], wf_d.rearrange("(k p) n -> p k n", p=P)),
                          "wf", 16)
        for m in range(4, 12):
            load_x(m)

        z = do("pool", lambda e: e.memset(ident[:, :], 0.0))
        tok["ident"] = do("pool", lambda e: e.affine_select(
            out=ident[:, :], in_=ident[:, :], compare_op=ALU.not_equal, fill=1.0, base=0,
            pattern=[[-1, P]], channel_multiplier=1), z)
        z = do("pool", lambda e: e.memset(causal[:, :], 1.0))
        tok["causal"] = do("pool", lambda e: e.affine_select(
            out=causal[:, :], in_=causal[:, :], compare_op=ALU.is_ge, fill=0.0, base=0,
            pattern=[[1, P]], channel_multiplier=-1), z)
        z = do("pool", lambda e: e.memset(blk[:, :], 0.0))
        for h in range(4):
            z = do("pool", lambda e, h=h: e.memset(blk[32 * h:32 * h + 32, 32 * h:32 * h + 32], 1.0), z)
        tok["blk"] = z

        def norm(src, dst, st, key, n, ready, reuse):
            row = st[:, n % 4, :]
            free = (tok[key, n - 4],) if n >= 4 else ()
            a = do("dve", lambda e: e.bn_stats(row[:, 0:6], src), ready, *free)
            a = do("dve", lambda e: e.bn_aggr(row[:, 6:8], row[:, 0:6]), a)
            do("dve", lambda e: e.tensor_scalar(row[:, 8:9], row[:, 6:7], -1.0, None, ALU.mult), a, tick=False)
            a = do("dve", lambda e: e.tensor_scalar(row[:, 9:10], row[:, 7:8], LN_EPS, None, ALU.add))
            a = do("pool", lambda e: e.tensor_tensor(row[:, 10:11], row[:, 9:10], half[:, :], ALU.pow), a, tok["half"])
            tok[key, n] = do("pool", lambda e: e.tensor_scalar(
                dst, src, row[:, 8:9], row[:, 10:11], ALU.add, ALU.mult), a, *reuse)

        def ln1(m):
            i = m % NX
            norm(xs[:, i, :], xn[:, m % 4, :], st1, "xn", m, tok["load", m],
                 (tok["t1", m - 4],) if m >= 4 else ())
            tok["xb", m] = do("pool", lambda e: e.tensor_tensor(xs[:, i, :], xs[:, i, :], bp[:, :], ALU.add),
                              tok["xn", m], tok["bias"])

        def t1(m):
            j, t = divmod(m, 4)
            r, free = take()
            tok["t1", m] = transposes(r, free, [xn[:, t, k * P:(k + 1) * P] for k in range(4)],
                                      tok["xn", m], tok["ident"])
            cols = slice(t * P, (t + 1) * P)
            reuse = (tok["qkv", j - 1, 8 + t],) if j else ()
            a = do("act", lambda e: e.activation(xth[:, :, cols], four(R[r][:, :]), ACT.Copy), tok["t1", m],
                   *reuse)
            b = do("dve", lambda e: e.tensor_tensor(xtl[:, :, cols], four(R[r][:, :]), xth[:, :, cols],
                                                    ALU.subtract), a, *reuse)
            tok["xt", m] = b
            give(r, a, b)

        def proj_qkv(j, i):
            dst = qkv[j % 2]
            r, free = take()
            mms = []
            last_use = (tok["av", 4 * j - 5],) if j >= 2 else ()
            if i < 8:
                cols = slice(i * P, (i + 1) * P)
                for k in range(4):
                    for a, b in ((wh, xth), (wh, xtl), (wl, xth)):
                        mms.append((R[r][:, :], a[:, k, cols], b[:, k, :], not mms, len(mms) == 11))
                tok["qkv", j, i] = group(r, free, mms, *(tok["xt", 4 * j + t] for t in range(4)), tok["w"])
                reuse = last_use + ((tok["qc", j - 2, i % 4],) if j >= 2 else ())
                e1 = do("act", lambda e: e.activation(dst[:, i, :], R[r][:, :], ACT.Exp, scale=wm[:, 5:6],
                                                      bias=bqk[:, i:i + 1]),
                        tok["qkv", j, i], tok["wm"], tok["bias"], *reuse)
                u = tok.get("nrel", 0)
                tok["nrel"] = u + 1
                a = do("act", lambda e: e.activation(rel[:, u % 2, :], R[r][:, :], ACT.Relu, scale=wm[:, 5:6],
                                                     bias=bqk[:, i:i + 1]),
                       *((tok["phi_n", u - 2],) if u >= 2 else ()))
                give(r, a)
                tok["phi", j, i] = tok["phi_n", u] = do("dve", lambda e: e.scalar_tensor_tensor(
                    dst[:, i, :], dst[:, i, :], 1.0, rel[:, u % 2, :], ALU.min, ALU.add), a)
            else:
                t = i - 8
                cols = slice(t * P, (t + 1) * P)
                for k in range(4):
                    for a, b in ((xth, wh), (xth, wl), (xtl, wh)):
                        mms.append((R[r][:, :], a[:, k, cols], b[:, k, 2 * D:], not mms, len(mms) == 11))
                tok["qkv", j, i] = group(r, free, mms, tok["xt", 4 * j + t], tok["w"])
                tok["v", j, t] = do("dve", lambda e: e.scalar_tensor_tensor(
                    dst[:, i, :], R[r][:, :], wm[:, 5:6], bv[:, :], ALU.mult, ALU.add),
                    tok["qkv", j, i], tok["wm"], tok["bias"], *last_use)
                give(r, tok["v", j, t])

        def denominators(j, g):
            src = qkv[j % 2]
            u = 4 * j + g
            c = cum[:, g % 2, :]
            start = 0.0 if j % 2 == 0 else carry[:, g:g + 1]
            a = do("dve", lambda e: e.tensor_tensor_scan(c, src[:, 4 + g, :], src[:, 4 + g, :], start,
                                                         ALU.add, ALU.bypass),
                   tok["phi", j, 4 + g], *((tok["qc_n", u - 2],) if u >= 2 else ()),
                   *((tok["carry", j - 1, g],) if j % 2 else ()))
            if j % 2 == 0:
                tok["carry", j, g] = do("dve", lambda e: e.tensor_copy(carry[:, g:g + 1], c[:, D - 1:D]), a)
                a = tok["carry", j, g]
            tok["qc", j, g] = tok["qc_n", u] = do("pool", lambda e: e.tensor_tensor(
                qc[:, g, :], c, src[:, g, :], ALU.mult), a, tok["phi", j, g],
                *((tok["den", 4 * j - 1],) if j else (tok["wft"],)))

        def parts(n):
            j, c = divmod(n, 4)
            return qkv[j % 2], j, c, slice(c * P, (c + 1) * P)

        def k_tokens(n):
            src, j, c, cols = parts(n)
            if n % PER == PER - 1:
                return
            r, free = take()
            a = transposes(r, free, [src[:, 4 + g, cols] for g in range(4)],
                           *(tok["phi", j, 4 + g] for g in range(4)))
            tok["ktok", n] = do("act", lambda e: e.activation(ktok[:, n % 2, :], R[r][:, :], ACT.Copy), a,
                                *((tok["delta", n - 2],) if ("delta", n - 2) in tok else ()))
            give(r, tok["ktok", n])

        def scores(n):
            src, j, c, cols = parts(n)
            mm = {}
            for g in range(4):
                for h in range(4):
                    rows = slice(32 * h, 32 * h + 32)
                    free = (tok["s_read", n - 1, h],) if n and g == 0 else ()
                    mm[h] = do("pe", lambda e, g=g, h=h, rows=rows: e.matmul(
                        S[h][:, g * P:(g + 1) * P], src[rows, 4 + g, cols], src[rows, g, cols],
                        start=True, stop=True),
                        tok["phi", j, g], tok["phi", j, 4 + g], *free, tick=g == 3)
            for h in range(4):
                reuse = (tok["av", n - 1],) if n else (tok["wpl"],)
                if h < 2:
                    tok["s_read", n, h] = tok["sm", n, h] = do("dve", lambda e, h=h: e.tensor_tensor(
                        four(sm[:, h, :]), four(S[h][:, :]), over(causal[:, :]), ALU.mult),
                        mm[h], tok["causal"], *reuse)
                else:
                    a = do("act", lambda e, h=h: e.activation(sm[:, h, :], S[h][:, :], ACT.Copy), mm[h], *reuse)
                    tok["s_read", n, h] = a
                    tok["sm", n, h] = do("pool", lambda e, h=h: e.affine_select(
                        out=four(sm[:, h, :]), in_=four(sm[:, h, :]), compare_op=ALU.is_ge, fill=0.0, base=0,
                        pattern=[[0, 4], [1, P]], channel_multiplier=-1), a)

        def update(n):
            src, j, c, cols = parts(n)
            if n % PER == PER - 1:
                return
            r, free = take()
            mms = [(R[r][:, g * P:(g + 1) * P], ktok[:, n % 2, g * P:(g + 1) * P],
                    src[:, 8 + c, g * P:(g + 1) * P], True, True) for g in range(4)]
            tok["delta", n] = group(r, free, mms, tok["ktok", n], tok["v", j, c])
            new = state[:, (n + 1) % 2, :]
            reuse = (tok["av", n - 1],) if n else ()
            if n % PER == 0:
                a = do("dve", lambda e: e.tensor_tensor(four(new), four(R[r][:, :]), over(blk[:, :]), ALU.mult),
                       tok["delta", n], tok["blk"], *reuse)
                tok["state", n + 1] = a
            else:
                a = do("dve", lambda e: e.tensor_tensor(four(delta[:, :]), four(R[r][:, :]), over(blk[:, :]),
                                                        ALU.mult),
                       tok["delta", n], *((tok["added"],) if "added" in tok else ()))
                tok["state", n + 1] = tok["added"] = do("pool", lambda e: e.tensor_tensor(
                    new, state[:, n % 2, :], delta[:, :], ALU.add), a, tok["state", n], *reuse)
            give(r, a)

        def den(n):
            src, j, c, cols = parts(n)
            r, free = take()
            mms = [(R[r][:, g * P:(g + 1) * P], blk[:, :], qc[:, g, cols], True, True) for g in range(4)]
            tok["den", n] = group(r, free, mms, tok["blk"], *(tok["qc", j, g] for g in range(4)))
            a = do("act", lambda e: e.activation(dene[:, :], R[r][:, :], ACT.Copy, bias=DEN_EPS), tok["den", n],
                   *((tok["rden", n - 1],) if n else ()))
            give(r, a)
            tok["rden", n] = do("dve", lambda e: e.reciprocal(rden[:, n % 2, :], dene[:, :]), a,
                                *((tok["y", n - 2],) if n >= 2 else ()))

        def values(n):
            src, j, c, cols = parts(n)
            first = n % PER == 0
            free = (tok["y", n - 1],) if n else ()
            if not first:
                for g in range(4):
                    do("pe", lambda e, g=g: e.matmul(
                        Y[:, g * P:(g + 1) * P], state[:, n % 2, g * P:(g + 1) * P], src[:, g, cols],
                        start=g == 0, stop=False, skip_group_check=True), tok["state", n], *free, tick=False)
            for g in range(4):
                for h in range(4):
                    col = (4 * g + h) * 32
                    a = do("pe", lambda e, g=g, h=h, col=col: e.matmul(
                        Y[32 * h:32 * h + 32, g * P:(g + 1) * P], src[:, 8 + c, col:col + 32],
                        sm[:, h, g * P:(g + 1) * P], start=first and g == 0, stop=True, skip_group_check=True),
                        tok["sm", n, h], tok["v", j, c], *free, tick=g == 3 and h == 3)
            tok["av", n] = a
            reuse = (tok["yl", n - 1], tok["yh", n - 1]) if n else ()
            tok["y", n] = do("dve", lambda e: e.tensor_tensor(y[:, :], Y[:, :], rden[:, n % 2, :], ALU.mult),
                             a, tok["rden", n], *reuse)
            reuse = (tok["proj", n - 2],) if n >= 2 else ()
            tok["yh", n] = do("act", lambda e: e.activation(yh[:, n % 2, :], y[:, :], ACT.Copy), tok["y", n], *reuse)
            tok["yl", n] = do("pool", lambda e: e.tensor_tensor(
                yl[:, n % 2, :], y[:, :], yh[:, n % 2, :].bitcast(F32), ALU.subtract), tok["yh", n], *reuse)

        def proj(n):
            r, free = take()
            mms = []
            for g in range(4):
                for a, b in ((yh, wph), (yh, wpl), (yl, wph)):
                    mms.append((R[r][:, :], a[:, n % 2, g * P:(g + 1) * P], b[:, g, :], not mms, len(mms) == 11))
            tok["proj", n] = group(r, free, mms, tok["yl", n], tok["wpl"])
            x = xs[:, n % NX, :]
            a = do("dve", lambda e: e.tensor_tensor(x, R[r][:, :], x, ALU.add), tok["proj", n], tok["xb", n])
            give(r, a)
            norm(x, x2[:, n % 2, :], st2, "x2", n, a, (tok["t2", n - 2],) if n >= 2 else ())
            tok["x1b", n] = do("pool", lambda e: e.tensor_tensor(x, x, bf[:, :], ALU.add), tok["x2", n])

        def t2(n):
            r, free = take()
            tok["t2", n] = transposes(r, free, [x2[:, n % 2, k * P:(k + 1) * P] for k in range(4)], tok["x2", n])
            tok["x2t", n] = do("act", lambda e: e.activation(x2t[:, n % 2, :], R[r][:, :], ACT.Copy, saturate=False),
                               tok["t2", n], *((tok["ffn", n - 2],) if n >= 2 else ()))
            give(r, tok["x2t", n])

        def ffn(n):
            r, free = take()
            mms = [(R[r][:, :], x2t[:, n % 2, k * P:(k + 1) * P], wft[:, k, :], k == 0, k == 3) for k in range(4)]
            tok["ffn", n] = group(r, free, mms, tok["x2t", n], tok["wft"])
            a = do("act", lambda e: e.activation(o16[:, n % 2, :], R[r][:, :], ACT.Copy), tok["ffn", n],
                   *((tok["out", n - 2],) if n >= 2 else ()))
            give(r, a)
            x = xs[:, n % NX, :]
            tok["out", n] = do("dve", lambda e: e.tensor_tensor(x, o16[:, n % 2, :], x, ALU.add), a, tok["x1b", n])
            tok["store", n] = q.dma("sp", lambda e: e.dma_start(out_d[n * P:(n + 1) * P, :], x),
                                    f"xo{n % NX}", 16 * (n // NX + 1), tok["out", n])

        flat = qkv[1][:, :, :].rearrange("p a n -> p (a n)")
        do("dve", lambda e: e.tensor_reduce(wm[:, 0:1], flat, AX.X, ALU.max), tok["wa"], tick=False)
        a = do("dve", lambda e: e.tensor_reduce(wm[:, 1:2], flat, AX.X, ALU.min))
        a = do("pool", lambda e: e.partition_all_reduce(wm[:, 2:4], wm[:, 0:2], P, bass.bass_isa.ReduceOp.absmax), a,
               tok["blk"])
        tok["half"] = do("pool", lambda e: e.memset(half[:, :], -0.5), a)
        for m in range(4):
            ln1(m)
        a = do("dve", lambda e: e.tensor_tensor(wm[:, 4:5], wm[:, 2:3], wm[:, 3:4], ALU.max), a)
        a = do("dve", lambda e: e.tensor_scalar(wm[:, 4:5], wm[:, 4:5], 2.0 ** -80, 2.0 ** 100, ALU.max, ALU.min), a)
        a = do("dve", lambda e: e.tensor_scalar(wm[:, 4:5].bitcast(I32), wm[:, 4:5].bitcast(I32), 0x7F800000, None,
                                                ALU.bitwise_and), a)
        tok["wm"] = do("dve", lambda e: e.tensor_scalar(wm[:, 5:6], wm[:, 4:5], 2.0 ** -13, None, ALU.mult), a)
        a = do("dve", lambda e: e.reciprocal(wm[:, 6:7], wm[:, 5:6]), tok["wm"])
        a = do("dve", lambda e: e.tensor_scalar(wh[:, :, :], raw, wm[:, 6:7], None, ALU.mult), a)
        tok["w"] = do("dve", lambda e: e.scalar_tensor_tensor(wl[:, :, :], raw, wm[:, 6:7], wh[:, :, :],
                                                              ALU.mult, ALU.subtract), a)
        for m in range(4):
            t1(m)
        a = do("act", lambda e: e.activation(wph[:, :, :], sm[:, :, :], ACT.Copy), tok["wp"])
        tok["wpl"] = do("dve", lambda e: e.tensor_tensor(wpl[:, :, :], sm[:, :, :], wph[:, :, :].bitcast(F32),
                                                         ALU.subtract), a)

        def ffn_weight():
            w = qc[:, :, :]
            lo = xn[:, 0, :].bitcast(F8).rearrange("p (k n) -> p k n", k=4)
            hi = xn[:, 1, :].bitcast(F8).rearrange("p (k n) -> p k n", k=4)
            tmp = qkv[1][:, 0:4, :]
            big = qkv[1][:, 4:8, :]
            free = [tok["t1", m] for m in range(4)]
            do("dve", lambda e: e.tensor_scalar(lo, w, 240.0, -240.0, ALU.min, ALU.max, saturate=False),
               tok["wf"], *free, tick=False)
            a = do("dve", lambda e: e.tensor_scalar(tmp, w, 0.5, 224.0, ALU.mult, ALU.min), tok["w"])
            a = do("dve", lambda e: e.tensor_scalar(hi, tmp, -224.0, None, ALU.max, saturate=False), a)
            b = do("dve", lambda e: e.tensor_tensor(big, w, w, ALU.mult))
            b = do("dve", lambda e: e.tensor_scalar(big, big, 128.0 * 128.0, None, ALU.is_gt), b)
            a = do("dve", lambda e: e.scalar_tensor_tensor(tmp, hi, 2.0, lo, ALU.mult, ALU.subtract), a)
            a = do("dve", lambda e: e.tensor_tensor(tmp, tmp, big, ALU.mult), a, b)
            a = do("dve", lambda e: e.tensor_tensor(w, tmp, lo, ALU.add), a)
            for k in range(4):
                r, free = take()
                b = transposes(r, free, [w[:, f, k * P:(k + 1) * P] for f in range(4)], a, tok["ident"])
                tok["wft"] = do("act", lambda e, r=r, k=k: e.activation(wft[:, k, :], R[r][:, :], ACT.Copy), b)
                give(r, tok["wft"])

        for i in range(6):
            proj_qkv(0, i)
        ffn_weight()
        for i in range(6, 12):
            proj_qkv(0, i)
        for m in range(4, 8):
            ln1(m)
        for g in range(4):
            denominators(0, g)

        for n in range(NT + 3):
            j, c = divmod(n, 4)
            if n < NT:
                more = j + 1 < NB
                if n + 12 < NT:
                    load_x(n + 12)
                if c == 0 and more:
                    for t in range(4):
                        t1(4 * j + 4 + t)
                if n + 8 < NT:
                    ln1(n + 8)
                k_tokens(n)
                scores(n)
                if more:
                    proj_qkv(j + 1, 3 * c)
                update(n)
                den(n)
                if more:
                    proj_qkv(j + 1, 3 * c + 1)
                values(n)
                if more:
                    proj_qkv(j + 1, 3 * c + 2)
                if c == 3 and more:
                    for g in range(4):
                        denominators(j + 1, g)
            if 3 <= n:
                ffn(n - 3)
            if 2 <= n < NT + 2:
                t2(n - 2)
            if 1 <= n < NT + 1:
                proj(n - 1)
        q.ops["sp"].append(([tok["store", n] for n in range(NT - NX, NT)], None, None))

        block = ctx.enter_context(nc.Block())

        @block.sync
        def _(e):
            last = q.ops["sp"].pop()
            q.run("sp", e, sems)
            for name, value in last[0]:
                e.wait_ge(sems[name], value)

        @block.scalar
        def _(e):
            q.run("act", e, sems)

        @block.vector
        def _(e):
            q.run("dve", e, sems)

        @block.gpsimd
        def _(e):
            q.run("pool", e, sems)

        @block.tensor
        def _(e):
            q.run("pe", e, sems)


_INS = ["L0_attn_x", "L0_attn_W_attn", "L0_attn_b_attn", "L0_attn_W_proj", "L0_attn_b_proj", "L0_ffn_weight",
        "L0_ffn_bias"]


def kernel(**inputs):
    import numpy as np
    import concourse.bacc as bacc
    from concourse.bass_utils import run_bass_kernel_spmd

    nc = bacc.Bacc("TRN2", target_bir_lowering=False, num_devices=1)
    arrays, args = {}, []
    for name in _INS:
        a = np.ascontiguousarray(inputs[name])
        if name == "L0_attn_x":
            a = a.reshape(B * T, D)
        arrays[f"in_{name}"] = a
        args.append(nc.dram_tensor(f"in_{name}", a.shape, mybir.dt.from_np(a.dtype), kind="ExternalInput").ap())
    args.append(nc.dram_tensor("out_0", (B * T, D), F32, kind="ExternalOutput").ap())
    build(nc, *args)
    r = run_bass_kernel_spmd(nc, [arrays], core_ids=[0])
    return r.results[0]["out_0"].reshape(B, T, D)
```

```python
from contextlib import ExitStack

import concourse.bass as bass
from concourse import mybir

ALU = mybir.AluOpType
ACT = mybir.ActivationFunctionType
AX = mybir.AxisListType
F32 = mybir.dt.float32
F16 = mybir.dt.float16
BF16 = mybir.dt.bfloat16
F8 = mybir.dt.float8e4
I32 = mybir.dt.int32

D = 512
B = 8
T = 1024
P = 128
NT = B * T // P
NB = NT // 4
PER = T // P
LN_EPS = 1e-5
DEN_EPS = 1e-6
NX = 16
NR = 3
MASK_DVE = 1


class Queues:

    ENGINES = ("pe", "act", "dve", "pool", "sp")

    def __init__(self):
        self.ops = {e: [] for e in self.ENGINES}
        self.count = {e: 0 for e in self.ENGINES}

    def do(self, eng, fn, *waits, tick=True):
        self.ops[eng].append((waits, fn, tick and (eng, 1)))
        if tick:
            self.count[eng] += 1
            return eng, self.count[eng]
        return None

    def dma(self, eng, fn, name, value, *waits):
        self.ops[eng].append((waits, fn, (name, 16)))
        return name, value

    def run(self, eng, e, sems):
        seen = {}
        for waits, fn, tick in self.ops[eng]:
            for name, value in waits:
                if seen.get(name, 0) < value:
                    e.wait_ge(sems[name], value)
                    seen[name] = value
            ins = fn(e)
            if tick:
                ins.then_inc(sems[tick[0]], tick[1])


def build(nc, x_d, wa_d, ba_d, wp_d, bp_d, wf_d, bf_d, out_d):
    ctx = ExitStack()
    with ctx:
        def sb(name, shape, dt):
            return ctx.enter_context(nc.sbuf_tensor(name, shape, dt))

        def psum(name):
            return ctx.enter_context(nc.psum_tensor(name, [P, 512], F32))

        xs = sb("xs", [P, NX, D], F32)
        xn = sb("xn", [P, 4, D], F32)
        xth = sb("xth", [P, 4, D], F16)
        xtl = sb("xtl", [P, 4, D], F16)
        qkv = [sb(f"qkv{i}", [P, 12, D], F32) for i in range(2)]
        ktok = sb("ktok", [P, 2, D], F32)
        rel = sb("rel", [P, 2, D], F32)
        sm = sb("sm", [P, 4, D], F32)
        state = sb("state", [P, 2, D], F32)
        delta = sb("delta", [P, D], F32)
        cum = sb("cum", [P, 2, D], F32)
        carry = sb("carry", [P, 4], F32)
        qc = sb("qc", [P, 4, D], F32)
        dene = sb("dene", [P, D], F32)
        rden = sb("rden", [P, 2, D], F32)
        y = sb("y", [P, D], F32)
        yh = sb("yh", [P, 2, D], F16)
        yl = sb("yl", [P, 2, D], F16)
        x2 = sb("x2", [P, 2, D], F32)
        x2t = sb("x2t", [P, 2, D], F8)
        o16 = sb("o16", [P, 2, D], F16)
        wh = sb("wh", [P, 4, 3 * D], F16)
        wl = sb("wl", [P, 4, 3 * D], F16)
        wph = sb("wph", [P, 4, D], F16)
        wpl = sb("wpl", [P, 4, D], F16)
        wft = sb("wft", [P, 4, D], BF16)
        causal = sb("causal", [P, P], BF16)
        blk = sb("blk", [P, P], F32)
        ident = sb("ident", [P, P], F32)
        bqk = sb("bqk", [P, 8], F32)
        bv = sb("bv", [P, D], F32)
        bp = sb("bp", [P, D], F32)
        bf = sb("bf", [P, D], F32)
        half = sb("half", [P, 1], F32)
        st1 = sb("st1", [P, 4, 12], F32)
        st2 = sb("st2", [P, 4, 12], F32)
        wm = sb("wm", [P, 24], F32)

        R = [psum(f"R{i}") for i in range(NR)]
        S = [psum(f"S{i}") for i in range(4)]
        Y = psum("Y")

        UP_W, UP_P = wm[:, 16:17], wm[:, 17:18]
        UN_W, UN_V, UN_P = wm[:, 14:15], wm[:, 22:23], wm[:, 23:24]

        q = Queues()
        do = q.do
        dma_sems = ["wa0", "wa1", "wa2", "wa3", "wp", "wf", "bias"] + [f"xi{i}" for i in range(NX)] + [f"xo{i}" for i in range(NX)]
        sems = {n: ctx.enter_context(nc.semaphore(f"s_{n}")) for n in [*Queues.ENGINES, *dma_sems]}

        tok = {}
        ring = {"n": 0, "free": [()] * NR}

        def take():
            r = ring["n"] % NR
            ring["n"] += 1
            return r, ring["free"][r]

        def give(r, *tokens):
            ring["free"][r] = tokens

        def group(r, frees, mms, *waits):
            last = None
            for i, (o, a, b, start, stop) in enumerate(mms):
                last = do("pe", lambda e, o=o, a=a, b=b, s=start, t=stop: e.matmul(
                    o, a, b, start=s, stop=t, skip_group_check=True),
                    *(waits if i == 0 else ()), *(frees if i == 0 else ()), tick=i == len(mms) - 1)
            return last

        def transposes(r, frees, ins, *waits):
            last = None
            for i, a in enumerate(ins):
                last = do("pe", lambda e, a=a, i=i: e.transpose(R[r][:, i * P:(i + 1) * P], a, ident[:, :]),
                          *(waits if i == 0 else ()), *(frees if i == 0 else ()), tick=i == len(ins) - 1)
            return last

        def four(t):
            return t.rearrange("p (g m) -> p g m", g=4)

        def over(t):
            return t.unsqueeze(1).broadcast_to([P, 4, P])

        def load_x(m):
            i = m % NX
            waits = (tok["store", m - NX],) if m >= NX else ()
            tok["load", m] = q.dma("sp", lambda e: e.dma_start(xs[:, i, :], x_d[m * P:(m + 1) * P, :]),
                                   f"xi{i}", 16 * (m // NX + 1), *waits)

        raw = qkv[1][:, :, :].rearrange("p a n -> p (a n)").rearrange("p (k n) -> p k n", k=4)
        for m in range(4):
            load_x(m)
        for k in range(4):
            tok["wa", k] = q.dma("act", lambda e, k=k: e.dma_start(raw[:, k, :], wa_d[k * P:(k + 1) * P, :]),
                                 f"wa{k}", 16)
        tok["wp"] = q.dma("act", lambda e: e.dma_start(sm[:, :, :], wp_d.rearrange("(k p) n -> p k n", p=P)),
                          "wp", 16)
        q.dma("act", lambda e: e.dma_start(bv[:, :], ba_d[2 * D:3 * D].partition_broadcast(P)), "bias", 16)
        q.dma("act", lambda e: e.dma_start(bqk[:, :], ba_d[0:2 * D].rearrange("(i p) -> p i", p=P),
                                           allow_slow_non_contiguous=True), "bias", 32)
        q.dma("act", lambda e: e.dma_start(bp[:, :], bp_d.partition_broadcast(P)), "bias", 48)
        tok["bias"] = q.dma("act", lambda e: e.dma_start(bf[:, :], bf_d.partition_broadcast(P)), "bias", 64)
        tok["wf"] = q.dma("act", lambda e: e.dma_start(qc[:, :, :], wf_d.rearrange("(k p) n -> p k n", p=P)),
                          "wf", 16)
        for m in range(4, 12):
            load_x(m)

        z = do("pool", lambda e: e.memset(ident[:, :], 0.0))
        tok["ident"] = do("pool", lambda e: e.affine_select(
            out=ident[:, :], in_=ident[:, :], compare_op=ALU.not_equal, fill=1.0, base=0,
            pattern=[[-1, P]], channel_multiplier=1), z)
        z = do("pool", lambda e: e.memset(causal[:, :], 1.0))
        tok["causal"] = do("pool", lambda e: e.affine_select(
            out=causal[:, :], in_=causal[:, :], compare_op=ALU.is_ge, fill=0.0, base=0,
            pattern=[[1, P]], channel_multiplier=-1), z)
        z = do("pool", lambda e: e.memset(blk[:, :], 0.0))
        for h in range(4):
            z = do("pool", lambda e, h=h: e.memset(blk[32 * h:32 * h + 32, 32 * h:32 * h + 32], 1.0), z)
        tok["blk"] = z
        tok["half"] = do("pool", lambda e: e.memset(half[:, :], -0.5), z)

        def norm(src, dst, st, key, n, ready, reuse):
            row = st[:, n % 4, :]
            free = (tok[key, n - 4],) if n >= 4 else ()
            a = do("dve", lambda e: e.bn_stats(row[:, 0:6], src), ready, *free)
            a = do("dve", lambda e: e.bn_aggr(row[:, 6:8], row[:, 0:6]), a)
            do("dve", lambda e: e.tensor_scalar(row[:, 8:9], row[:, 6:7], -1.0, None, ALU.mult), a, tick=False)
            a = do("dve", lambda e: e.tensor_scalar(row[:, 9:10], row[:, 7:8], LN_EPS, None, ALU.add))
            a = do("pool", lambda e: e.tensor_tensor(row[:, 10:11], row[:, 9:10], half[:, :], ALU.pow), a, tok["half"])
            tok[key, n] = do("pool", lambda e: e.tensor_scalar(
                dst, src, row[:, 8:9], row[:, 10:11], ALU.add, ALU.mult), a, *reuse)

        def ln1(m):
            i = m % NX
            norm(xs[:, i, :], xn[:, m % 4, :], st1, "xn", m, tok["load", m],
                 (tok["t1", m - 4],) if m >= 4 else ())

        def add_bp(m):
            i = m % NX
            tok["xb", m] = do("pool", lambda e: e.tensor_tensor(xs[:, i, :], xs[:, i, :], bp[:, :], ALU.add),
                              tok["xn", m], tok["bias"])

        def t1(m):
            j, t = divmod(m, 4)
            r, free = take()
            tok["t1", m] = transposes(r, free, [xn[:, t, k * P:(k + 1) * P] for k in range(4)],
                                      tok["xn", m], tok["ident"])
            cols = slice(t * P, (t + 1) * P)
            reuse = (tok["qkv", j - 1, 8 + t],) if j else ()
            a = do("act", lambda e: e.activation(xth[:, :, cols], four(R[r][:, :]), ACT.Copy), tok["t1", m],
                   *reuse)
            b = do("dve", lambda e: e.tensor_tensor(xtl[:, :, cols], four(R[r][:, :]), xth[:, :, cols],
                                                    ALU.subtract), a, *reuse)
            tok["xt", m] = b
            give(r, a, b)

        def proj_qkv(j, i):
            dst = qkv[j % 2]
            r, free = take()
            mms = []
            last_use = (tok["av", 4 * j - 5],) if j >= 2 else ()
            if i < 8:
                cols = slice(i * P, (i + 1) * P)
                for k in range(4):
                    for a, b in ((wh, xth), (wh, xtl), (wl, xth)):
                        mms.append((R[r][:, :], a[:, k, cols], b[:, k, :], not mms, len(mms) == 11))
                tok["qkv", j, i] = group(r, free, mms, *(tok["xt", 4 * j + t] for t in range(4)), tok["w", i // 4])
                reuse = last_use + ((tok["qc", j - 2, i % 4],) if j >= 2 else ())
                e1 = do("act", lambda e: e.activation(dst[:, i, :], R[r][:, :], ACT.Exp, scale=UN_W,
                                                      bias=bqk[:, i:i + 1]),
                        tok["qkv", j, i], tok["scales"], tok["bias"], *reuse)
                u = tok.get("nrel", 0)
                tok["nrel"] = u + 1
                a = do("act", lambda e: e.activation(rel[:, u % 2, :], R[r][:, :], ACT.Relu, scale=UN_W,
                                                     bias=bqk[:, i:i + 1]),
                       *((tok["phi_n", u - 2],) if u >= 2 else ()))
                give(r, a)
                tok["phi", j, i] = tok["phi_n", u] = do("dve", lambda e: e.scalar_tensor_tensor(
                    dst[:, i, :], dst[:, i, :], 1.0, rel[:, u % 2, :], ALU.min, ALU.add), a)
            else:
                t = i - 8
                cols = slice(t * P, (t + 1) * P)
                for k in range(4):
                    for a, b in ((xth, wh), (xth, wl), (xtl, wh)):
                        mms.append((R[r][:, :], a[:, k, cols], b[:, k, 2 * D:], not mms, len(mms) == 11))
                tok["qkv", j, i] = group(r, free, mms, tok["xt", 4 * j + t], tok["w", 2])
                tok["v", j, t] = do("dve", lambda e: e.scalar_tensor_tensor(
                    dst[:, i, :], R[r][:, :], UN_V, bv[:, :], ALU.mult, ALU.add),
                    tok["qkv", j, i], tok["scales"], tok["bv"], *last_use)
                give(r, tok["v", j, t])

        def denominators(j, g):
            src = qkv[j % 2]
            u = 4 * j + g
            c = cum[:, g % 2, :]
            start = 0.0 if j % 2 == 0 else carry[:, g:g + 1]
            a = do("dve", lambda e: e.tensor_tensor_scan(c, src[:, 4 + g, :], src[:, 4 + g, :], start,
                                                         ALU.add, ALU.bypass),
                   tok["phi", j, 4 + g], *((tok["qc_n", u - 2],) if u >= 2 else ()),
                   *((tok["carry", j - 1, g],) if j % 2 else ()))
            if j % 2 == 0:
                tok["carry", j, g] = do("dve", lambda e: e.tensor_copy(carry[:, g:g + 1], c[:, D - 1:D]), a)
                a = tok["carry", j, g]
            tok["qc", j, g] = tok["qc_n", u] = do("pool", lambda e: e.tensor_tensor(
                qc[:, g, :], c, src[:, g, :], ALU.mult), a, tok["phi", j, g],
                *((tok["den", 4 * j - 1],) if j else (tok["wft"],)))

        def parts(n):
            j, c = divmod(n, 4)
            return qkv[j % 2], j, c, slice(c * P, (c + 1) * P)

        def k_tokens(n):
            src, j, c, cols = parts(n)
            if n % PER == PER - 1:
                return
            r, free = take()
            a = transposes(r, free, [src[:, 4 + g, cols] for g in range(4)],
                           *(tok["phi", j, 4 + g] for g in range(4)))
            tok["ktok", n] = do("act", lambda e: e.activation(ktok[:, n % 2, :], R[r][:, :], ACT.Copy), a,
                                *((tok["delta", n - 2],) if ("delta", n - 2) in tok else ()))
            give(r, tok["ktok", n])

        def scores(n, groups):
            src, j, c, cols = parts(n)
            mm = {}
            for g in groups:
                for h in range(4):
                    rows = slice(32 * h, 32 * h + 32)
                    free = (tok["s_read", n - 1, h],) if n and g == 0 else ()
                    mm[h] = do("pe", lambda e, g=g, h=h, rows=rows: e.matmul(
                        S[h][:, g * P:(g + 1) * P], src[rows, 4 + g, cols], src[rows, g, cols],
                        start=True, stop=True),
                        tok["phi", j, g], tok["phi", j, 4 + g], *free, tick=g == 3)
            if 3 not in groups:
                return
            for h in range(4):
                reuse = (tok["av", n - 1],) if n else (tok["wpl"],)
                if h < MASK_DVE:
                    tok["s_read", n, h] = tok["sm", n, h] = do("dve", lambda e, h=h: e.tensor_tensor(
                        four(sm[:, h, :]), four(S[h][:, :]), over(causal[:, :]), ALU.mult),
                        mm[h], tok["causal"], *reuse)
                else:
                    a = do("act", lambda e, h=h: e.activation(sm[:, h, :], S[h][:, :], ACT.Copy), mm[h], *reuse)
                    tok["s_read", n, h] = a
                    tok["sm", n, h] = do("pool", lambda e, h=h: e.affine_select(
                        out=four(sm[:, h, :]), in_=four(sm[:, h, :]), compare_op=ALU.is_ge, fill=0.0, base=0,
                        pattern=[[0, 4], [1, P]], channel_multiplier=-1), a)

        def update(n):
            src, j, c, cols = parts(n)
            if n % PER == PER - 1:
                return
            r, free = take()
            mms = [(R[r][:, g * P:(g + 1) * P], ktok[:, n % 2, g * P:(g + 1) * P],
                    src[:, 8 + c, g * P:(g + 1) * P], True, True) for g in range(4)]
            tok["delta", n] = group(r, free, mms, tok["ktok", n], tok["v", j, c])
            new = state[:, (n + 1) % 2, :]
            reuse = (tok["av", n - 1],) if n else ()
            if n % PER == 0:
                a = do("dve", lambda e: e.tensor_tensor(four(new), four(R[r][:, :]), over(blk[:, :]), ALU.mult),
                       tok["delta", n], tok["blk"], *reuse)
                tok["state", n + 1] = a
            else:
                a = do("dve", lambda e: e.tensor_tensor(four(delta[:, :]), four(R[r][:, :]), over(blk[:, :]),
                                                        ALU.mult),
                       tok["delta", n], *((tok["added"],) if "added" in tok else ()))
                tok["state", n + 1] = tok["added"] = do("pool", lambda e: e.tensor_tensor(
                    new, state[:, n % 2, :], delta[:, :], ALU.add), a, tok["state", n], *reuse)
            give(r, a)

        def den(n):
            src, j, c, cols = parts(n)
            r, free = take()
            mms = [(R[r][:, g * P:(g + 1) * P], blk[:, :], qc[:, g, cols], True, True) for g in range(4)]
            tok["den", n] = group(r, free, mms, tok["blk"], *(tok["qc", j, g] for g in range(4)))
            a = do("act", lambda e: e.activation(dene[:, :], R[r][:, :], ACT.Copy, bias=DEN_EPS), tok["den", n],
                   *((tok["rden", n - 1],) if n else ()))
            give(r, a)
            tok["dene", n] = a

        def invert(n, g):
            cols = slice(g * P, (g + 1) * P)
            tok["rden", n] = do("dve", lambda e: e.reciprocal(rden[:, n % 2, cols], dene[:, cols]), tok["dene", n],
                                *((tok["y", n - 2],) if n >= 2 else ()))

        def values(n):
            src, j, c, cols = parts(n)
            first = n % PER == 0
            free = (tok["y", n - 1],) if n else ()
            if not first:
                for g in range(4):
                    do("pe", lambda e, g=g: e.matmul(
                        Y[:, g * P:(g + 1) * P], state[:, n % 2, g * P:(g + 1) * P], src[:, g, cols],
                        start=g == 0, stop=False, skip_group_check=True), tok["state", n], *free, tick=False)
            for g in range(4):
                for h in range(4):
                    col = (4 * g + h) * 32
                    a = do("pe", lambda e, g=g, h=h, col=col: e.matmul(
                        Y[32 * h:32 * h + 32, g * P:(g + 1) * P], src[:, 8 + c, col:col + 32],
                        sm[:, h, g * P:(g + 1) * P], start=first and g == 0, stop=True, skip_group_check=True),
                        tok["sm", n, h], tok["v", j, c], *free, tick=g == 3 and h == 3)
            tok["av", n] = a
            reuse = (tok["yl", n - 1], tok["yh", n - 1]) if n else ()
            tok["y", n] = do("dve", lambda e: e.tensor_tensor(y[:, :], Y[:, :], rden[:, n % 2, :], ALU.mult),
                             a, tok["rden", n], *reuse)
            reuse = (tok["proj", n - 2],) if n >= 2 else ()
            tok["yh", n] = do("act", lambda e: e.activation(yh[:, n % 2, :], y[:, :], ACT.Copy), tok["y", n], *reuse)
            tok["yl", n] = do("pool", lambda e: e.tensor_tensor(
                yl[:, n % 2, :], y[:, :], yh[:, n % 2, :], ALU.subtract), tok["yh", n], *reuse)

        def proj(n):
            r, free = take()
            mms = []
            for g in range(4):
                for a, b in ((yh, wph), (yh, wpl), (yl, wph)):
                    mms.append((R[r][:, :], a[:, n % 2, g * P:(g + 1) * P], b[:, g, :], not mms, len(mms) == 11))
            tok["proj", n] = group(r, free, mms, tok["yl", n], tok["wpl"])
            x = xs[:, n % NX, :]
            a = do("dve", lambda e: e.scalar_tensor_tensor(x, R[r][:, :], UN_P, x, ALU.mult, ALU.add),
                   tok["proj", n], tok["xb", n])
            give(r, a)
            norm(x, x2[:, n % 2, :], st2, "x2", n, a, (tok["t2", n - 2],) if n >= 2 else ())
            tok["x1b", n] = do("pool", lambda e: e.tensor_tensor(x, x, bf[:, :], ALU.add), tok["x2", n])

        def t2(n):
            r, free = take()
            tok["t2", n] = transposes(r, free, [x2[:, n % 2, k * P:(k + 1) * P] for k in range(4)], tok["x2", n])
            tok["x2t", n] = do("act", lambda e: e.activation(x2t[:, n % 2, :], R[r][:, :], ACT.Copy, saturate=False),
                               tok["t2", n], *((tok["ffn", n - 2],) if n >= 2 else ()))
            give(r, tok["x2t", n])

        def ffn(n):
            r, free = take()
            mms = [(R[r][:, :], x2t[:, n % 2, k * P:(k + 1) * P], wft[:, k, :], k == 0, k == 3) for k in range(4)]
            tok["ffn", n] = group(r, free, mms, tok["x2t", n], tok["wft"])
            a = do("act", lambda e: e.activation(o16[:, n % 2, :], R[r][:, :], ACT.Copy), tok["ffn", n],
                   *((tok["out", n - 2],) if n >= 2 else ()))
            give(r, a)
            x = xs[:, n % NX, :]
            tok["out", n] = do("dve", lambda e: e.tensor_tensor(x, o16[:, n % 2, :], x, ALU.add), a, tok["x1b", n])
            tok["store", n] = q.dma("sp", lambda e: e.dma_start(out_d[n * P:(n + 1) * P, :], x),
                                    f"xo{n % NX}", 16 * (n // NX + 1), tok["out", n])

        def pow2(dst, src, *waits):
            return do("dve", lambda e: e.tensor_scalar(dst.bitcast(I32), src.bitcast(I32), 0x7F800000, None,
                                                       ALU.bitwise_and), *waits)

        def scales():
            b = tok["wp"]
            for k in range(4):
                do("dve", lambda e, k=k: e.tensor_reduce(wm[:, k:k + 1], raw[:, k, :], AX.X, ALU.max,
                                                         apply_absolute_value=True), tok["wa", k], tick=False)
            do("dve", lambda e: e.tensor_reduce(wm[:, 4:5], bv[:, :], AX.X, ALU.max, apply_absolute_value=True),
               tok["bias"], tick=False)
            a = do("dve", lambda e: e.tensor_reduce(wm[:, 7:8], sm[:, :, :].rearrange("p k n -> p (k n)"), AX.X,
                                                    ALU.max, apply_absolute_value=True), b)
            a = do("dve", lambda e: e.tensor_reduce(wm[:, 6:7], wm[:, 0:4], AX.X, ALU.max), a)
            a = do("pool", lambda e: e.partition_all_reduce(wm[:, 8:10], wm[:, 6:8], P,
                                                            bass.bass_isa.ReduceOp.absmax), a, tok["blk"])
            tok["reduced"] = a
            a = do("dve", lambda e: e.tensor_scalar(wm[:, 10:12], wm[:, 8:10], 2.0 ** -80, 2.0 ** 80, ALU.max,
                                                    ALU.min), a)
            a = pow2(wm[:, 12:14], wm[:, 10:12], a)
            a = do("dve", lambda e: e.tensor_scalar(wm[:, 14:16], wm[:, 12:14], 2.0 ** -13, None, ALU.mult), a)
            tok["up"] = do("dve", lambda e: e.reciprocal(wm[:, 16:18], wm[:, 14:16]), a)
            a = do("dve", lambda e: e.scalar_tensor_tensor(wm[:, 18:19], wm[:, 12:13], 2.0 * D, wm[:, 4:5],
                                                           ALU.mult, ALU.add))
            a = pow2(wm[:, 19:20], wm[:, 18:19], a)
            a = do("dve", lambda e: e.tensor_scalar(wm[:, 20:21], wm[:, 19:20], 2.0 ** -14, None, ALU.mult), a)
            a = do("dve", lambda e: e.reciprocal(wm[:, 21:22], wm[:, 20:21]), a)
            do("dve", lambda e: e.tensor_tensor(wm[:, 22:23], wm[:, 14:15], wm[:, 21:22], ALU.mult), a, tick=False)
            do("dve", lambda e: e.tensor_tensor(wm[:, 23:24], wm[:, 15:16], wm[:, 20:21], ALU.mult), tick=False)
            tok["scales"] = tok["bv"] = do("dve", lambda e: e.tensor_scalar(bv[:, :], bv[:, :], wm[:, 21:22], None,
                                                                            ALU.mult))

        for m in range(4):
            ln1(m)
        for m in range(4):
            t1(m)
        scales()
        for m in range(4):
            add_bp(m)
        for i in range(3):
            cols = slice(i * D, (i + 1) * D)
            a = do("act", lambda e, cols=cols: e.activation(wh[:, :, cols], raw[:, :, cols], ACT.Copy, scale=UP_W),
                   tok["up"])
            tok["w", i] = do("dve", lambda e, cols=cols: e.scalar_tensor_tensor(
                wl[:, :, cols], raw[:, :, cols], UP_W, wh[:, :, cols], ALU.mult, ALU.subtract), a)
        a = do("act", lambda e: e.activation(wph[:, :, :], sm[:, :, :], ACT.Copy, scale=UP_P), tok["up"])
        tok["wpl"] = do("dve", lambda e: e.scalar_tensor_tensor(wpl[:, :, :], sm[:, :, :], UP_P, wph[:, :, :],
                                                                ALU.mult, ALU.subtract), a)

        def ffn_weight():
            w = qc[:, :, :]
            lo = xn[:, 0, :].bitcast(F8).rearrange("p (k n) -> p k n", k=4)
            hi = xn[:, 1, :].bitcast(F8).rearrange("p (k n) -> p k n", k=4)
            tmp = qkv[1][:, 0:4, :]
            big = qkv[1][:, 4:8, :]
            a = do("dve", lambda e: e.tensor_scalar(lo, w, 240.0, -240.0, ALU.min, ALU.max, saturate=False),
                   tok["wf"], tok["t1", 0])
            yield
            a = do("dve", lambda e: e.tensor_scalar(tmp, w, 0.5, 224.0, ALU.mult, ALU.min), tok["w", 2])
            yield
            a = do("dve", lambda e: e.tensor_scalar(hi, tmp, -224.0, None, ALU.max, saturate=False), a,
                   tok["t1", 1])
            yield
            b = do("dve", lambda e: e.tensor_tensor(big, w, w, ALU.mult))
            yield
            b = do("dve", lambda e: e.tensor_scalar(big, big, 128.0 * 128.0, None, ALU.is_gt), b)
            yield
            a = do("dve", lambda e: e.scalar_tensor_tensor(tmp, hi, 2.0, lo, ALU.mult, ALU.subtract), a)
            yield
            a = do("dve", lambda e: e.tensor_tensor(tmp, tmp, big, ALU.mult), a, b)
            yield
            a = do("dve", lambda e: e.tensor_tensor(w, tmp, lo, ALU.add), a)
            yield
            for k in range(4):
                r, free = take()
                b = transposes(r, free, [w[:, f, k * P:(k + 1) * P] for f in range(4)], a, tok["ident"])
                tok["wft"] = do("act", lambda e, r=r, k=k: e.activation(wft[:, k, :], R[r][:, :], ACT.Copy), b)
                give(r, tok["wft"])
            yield

        weight = ffn_weight()
        for i in range(8):
            proj_qkv(0, i)
            next(weight)
        for t in range(4):
            ln1(4 + t)
            add_bp(4 + t)
            proj_qkv(0, 8 + t)
            t1(4 + t)
            if t == 0:
                next(weight)
        for g in range(4):
            denominators(0, g)

        k_tokens(0)
        for n in range(NT + 3):
            j, c = divmod(n, 4)
            if n < NT:
                more = j + 1 < NB
                if n + 12 < NT:
                    load_x(n + 12)
                ahead = c == 3 and j + 2 < NB
                if n + 8 < NT:
                    ln1(n + 8)
                    add_bp(n + 8)
                scores(n, (0, 1))
                if ahead:
                    t1(4 * j + 8)
                if more:
                    proj_qkv(j + 1, 3 * c)
                scores(n, (2, 3))
                if ahead:
                    t1(4 * j + 9)
                den(n)
                if more:
                    proj_qkv(j + 1, 3 * c + 1)
                invert(n, 0)
                if c == 3 and more:
                    for g in range(2):
                        denominators(j + 1, g)
                if ahead:
                    t1(4 * j + 10)
                invert(n, 1)
                update(n)
                invert(n, 2)
                if n + 1 < NT:
                    k_tokens(n + 1)
                if more:
                    proj_qkv(j + 1, 3 * c + 2)
                invert(n, 3)
                values(n)
                if c == 3 and more:
                    for g in range(2, 4):
                        denominators(j + 1, g)
                if ahead:
                    t1(4 * j + 11)
            if 3 <= n:
                ffn(n - 3)
            if 1 <= n < NT + 1:
                proj(n - 1)
            if 2 <= n < NT + 2:
                t2(n - 2)
        q.ops["sp"].append(([tok["store", n] for n in range(NT - NX, NT)], None, None))

        block = ctx.enter_context(nc.Block())

        @block.sync
        def _(e):
            last = q.ops["sp"].pop()
            q.run("sp", e, sems)
            for name, value in last[0]:
                e.wait_ge(sems[name], value)

        @block.scalar
        def _(e):
            q.run("act", e, sems)

        @block.vector
        def _(e):
            q.run("dve", e, sems)

        @block.gpsimd
        def _(e):
            q.run("pool", e, sems)

        @block.tensor
        def _(e):
            q.run("pe", e, sems)


_INS = ["L0_attn_x", "L0_attn_W_attn", "L0_attn_b_attn", "L0_attn_W_proj", "L0_attn_b_proj", "L0_ffn_weight",
        "L0_ffn_bias"]


def kernel(**inputs):
    import numpy as np
    import concourse.bacc as bacc
    from concourse.bass_utils import run_bass_kernel_spmd

    nc = bacc.Bacc("TRN2", target_bir_lowering=False, num_devices=1)
    arrays, args = {}, []
    for name in _INS:
        a = np.ascontiguousarray(inputs[name])
        if name == "L0_attn_x":
            a = a.reshape(B * T, D)
        arrays[f"in_{name}"] = a
        args.append(nc.dram_tensor(f"in_{name}", a.shape, mybir.dt.from_np(a.dtype), kind="ExternalInput").ap())
    args.append(nc.dram_tensor("out_0", (B * T, D), F32, kind="ExternalOutput").ap())
    build(nc, *args)
    r = run_bass_kernel_spmd(nc, [arrays], core_ids=[0])
    return r.results[0]["out_0"].reshape(B, T, D)
```

```python
from contextlib import ExitStack

import concourse.bass as bass
from concourse import mybir

ALU = mybir.AluOpType
ACT = mybir.ActivationFunctionType
AX = mybir.AxisListType
F32 = mybir.dt.float32
F32R = mybir.dt.float32r
F16 = mybir.dt.float16
BF16 = mybir.dt.bfloat16
F8 = mybir.dt.float8e4
I32 = mybir.dt.int32

D = 512
B = 8
T = 1024
P = 128
NT = B * T // P
NB = NT // 4
PER = T // P
LN_EPS = 1e-5
DEN_EPS = 1e-6
NX = 14
NR = 3
MASK_DVE = 1


class Queues:

    ENGINES = ("pe", "act", "dve", "pool", "sp")

    def __init__(self):
        self.ops = {e: [] for e in self.ENGINES}
        self.count = {e: 0 for e in self.ENGINES}

    def do(self, eng, fn, *waits, tick=True):
        self.ops[eng].append((waits, fn, tick and (eng, 1)))
        if tick:
            self.count[eng] += 1
            return eng, self.count[eng]
        return None

    def dma(self, eng, fn, name, value, *waits):
        self.ops[eng].append((waits, fn, (name, 16)))
        return name, value

    def run(self, eng, e, sems):
        seen = {}
        for waits, fn, tick in self.ops[eng]:
            for name, value in waits:
                if seen.get(name, 0) < value:
                    e.wait_ge(sems[name], value)
                    seen[name] = value
            ins = fn(e)
            if tick:
                ins.then_inc(sems[tick[0]], tick[1])


def build(nc, x_d, wa_d, ba_d, wp_d, bp_d, wf_d, bf_d, out_d):
    ctx = ExitStack()
    with ctx:
        def sb(name, shape, dt):
            return ctx.enter_context(nc.sbuf_tensor(name, shape, dt))

        def psum(name):
            return ctx.enter_context(nc.psum_tensor(name, [P, 512], F32))

        xs = sb("xs", [P, NX, D], F32)
        xn = sb("xn", [P, 2, D], F32)
        xnhl = sb("xnhl", [P, 4, 2, D], F16)
        xt = sb("xt", [P, 8, D], F16)
        qkv = [sb(f"qkv{i}", [P, 12, D], F32) for i in range(2)]
        ktok = sb("ktok", [P, 2, D], F32)
        rel = sb("rel", [P, 2, D], F32)
        sm = sb("sm", [P, 4, D], F32)
        state = sb("state", [P, 2, D], F32)
        cum = sb("cum", [P, 2, D], F32)
        carry = sb("carry", [P, 4], F32)
        qch = sb("qch", [P, D], F32R)
        qcl = sb("qcl", [P, D], F32R)
        rden = [sb(f"rden{i}", [P, 4, D], F32) for i in range(2)]
        y = sb("y", [P, D], F32)
        yh = sb("yh", [P, 2, D], F16)
        yl = sb("yl", [P, 2, D], F16)
        x2 = sb("x2", [P, 2, D], F32)
        x28 = sb("x28", [P, D], F8)
        x2b = sb("x2b", [P, 2, D], BF16)
        x2t = sb("x2t", [P, 2, 4, P], BF16)
        o16 = sb("o16", [P, 2, D], F16)
        wh = sb("wh", [P, 4, 3 * D], F16)
        wl = sb("wl", [P, 4, 3 * D], F16)
        wph = sb("wph", [P, 4, D], F16)
        wpl = sb("wpl", [P, 4, D], F16)
        wft = sb("wft", [P, 4, D], BF16)
        causal = sb("causal", [P, P], BF16)
        blk = sb("blk", [P, P], F32)
        blkr = sb("blkr", [P, P], F32R)
        ident = sb("ident", [P, P], F32)
        bqk = sb("bqk", [P, 8], F32)
        bv = sb("bv", [P, D], F32)
        bp = sb("bp", [P, D], F32)
        bf = sb("bf", [P, D], F32)
        half = sb("half", [P, 1], F32)
        st1 = sb("st1", [P, 4, 12], F32)
        st2 = sb("st2", [P, 4, 12], F32)
        wm = sb("wm", [P, 26], F32)

        R = [psum(f"R{i}") for i in range(NR)]
        S = [psum(f"S{i}") for i in range(4)]
        Y = psum("Y")

        xth, xtl = xt[:, 0:4, :], xt[:, 4:8, :]
        UP_W, UP_P = wm[:, 5:6], wm[:, 12:13]
        UN_W, UN_V, UN_P = wm[:, 4:5], wm[:, 19:20], wm[:, 24:25]

        q = Queues()
        do = q.do
        dma_sems = ["wa0", "wa1", "wa2", "wa3", "wp", "wf", "bias", "xt0", "xt1", "xt2", "xt3", "x2t0", "x2t1"] + [f"xi{i}" for i in range(NX)] + [f"xo{i}" for i in range(NX)]
        sems = {n: ctx.enter_context(nc.semaphore(f"s_{n}")) for n in [*Queues.ENGINES, *dma_sems]}

        tok = {}
        ring = {"n": 0, "free": [()] * NR}

        def take():
            r = ring["n"] % NR
            ring["n"] += 1
            return r, ring["free"][r]

        def give(r, *tokens):
            ring["free"][r] = tokens

        def group(r, frees, mms, *waits):
            last = None
            for i, (o, a, b, start, stop) in enumerate(mms):
                last = do("pe", lambda e, o=o, a=a, b=b, s=start, t=stop: e.matmul(
                    o, a, b, start=s, stop=t, skip_group_check=True),
                    *(waits if i == 0 else ()), *(frees if i == 0 else ()), tick=i == len(mms) - 1)
            return last

        def transposes(bank, frees, ins, *waits):
            last = None
            for i, a in enumerate(ins):
                last = do("pe", lambda e, a=a, i=i: e.transpose(bank[:, i * P:(i + 1) * P], a, ident[:, :]),
                          *(waits if i == 0 else ()), *(frees if i == 0 else ()), tick=i == len(ins) - 1)
            return last

        def four(t):
            return t.rearrange("p (g m) -> p g m", g=4)

        def over(t):
            return t.unsqueeze(1).broadcast_to([P, 4, P])

        def load_x(m):
            i = m % NX
            waits = (tok["store", m - NX],) if m >= NX else (tok["wpl"],) if m >= NX - 4 else ()
            tok["load", m] = q.dma("sp", lambda e: e.dma_start(xs[:, i, :], x_d[m * P:(m + 1) * P, :]),
                                   f"xi{i}", 16 * (m // NX + 1), *waits)

        raw = qkv[1][:, :, :].rearrange("p a n -> p (a n)").rearrange("p (k n) -> p k n", k=4)
        raw_p = xs[:, NX - 4:NX, :]
        x32 = sm
        for m in range(4):
            load_x(m)
        for k in range(4):
            tok["wa", k] = q.dma("sp", lambda e, k=k: e.dma_start(raw[:, k, :], wa_d[k * P:(k + 1) * P, :]),
                                 f"wa{k}", 16)
        q.dma("act", lambda e: e.dma_start(bqk[:, :], ba_d[0:2 * D].rearrange("(i p) -> p i", p=P),
                                           allow_slow_non_contiguous=True), "bias", 16)
        q.dma("act", lambda e: e.dma_start(bp[:, :], bp_d.partition_broadcast(P)), "bias", 32)
        q.dma("act", lambda e: e.dma_start(bv[:, :], ba_d[2 * D:3 * D].partition_broadcast(P)), "bias", 48)
        tok["bias"] = q.dma("act", lambda e: e.dma_start(bf[:, :], bf_d.partition_broadcast(P)), "bias", 64)
        tok["wf"] = q.dma("sp", lambda e: e.dma_start(rden[1][:, :, :], wf_d.rearrange("(k p) n -> p k n", p=P)),
                          "wf", 16)
        for m in range(4, 10):
            load_x(m)
        tok["wp"] = q.dma("sp", lambda e: e.dma_start(raw_p, wp_d.rearrange("(k p) n -> p k n", p=P)),
                          "wp", 16)

        z = do("pool", lambda e: e.memset(ident[:, :], 0.0))
        tok["ident"] = do("pool", lambda e: e.affine_select(
            out=ident[:, :], in_=ident[:, :], compare_op=ALU.not_equal, fill=1.0, base=0,
            pattern=[[-1, P]], channel_multiplier=1), z)
        z = do("pool", lambda e: e.memset(causal[:, :], 1.0))
        tok["causal"] = do("pool", lambda e: e.affine_select(
            out=causal[:, :], in_=causal[:, :], compare_op=ALU.is_ge, fill=0.0, base=0,
            pattern=[[1, P]], channel_multiplier=-1), z)
        z = do("pool", lambda e: e.memset(blk[:, :], 0.0))
        for h in range(4):
            z = do("pool", lambda e, h=h: e.memset(blk[32 * h:32 * h + 32, 32 * h:32 * h + 32], 1.0), z)
        tok["blk"] = z
        tok["zeros"] = do("pool", lambda e: e.memset(state[:, :, :], 0.0), z)
        tok["blkr"] = do("act", lambda e: e.activation(blkr[:, :], blk[:, :], ACT.Copy), z)
        tok["half"] = do("pool", lambda e: e.memset(half[:, :], -0.5), z)

        def norm(src, dst, st, key, n, ready, reuse):
            row = st[:, n % 4, :]
            free = (tok[key, n - 4],) if n >= 4 else ()
            a = do("dve", lambda e: e.bn_stats(row[:, 0:6], src), ready, *free)
            a = do("dve", lambda e: e.bn_aggr(row[:, 6:8], row[:, 0:6]), a)
            do("dve", lambda e: e.tensor_scalar(row[:, 8:9], row[:, 6:7], -1.0, None, ALU.mult), a, tick=False)
            a = do("dve", lambda e: e.tensor_scalar(row[:, 9:10], row[:, 7:8], LN_EPS, None, ALU.add))
            a = do("pool", lambda e: e.tensor_tensor(row[:, 10:11], row[:, 9:10], half[:, :], ALU.pow), a, tok["half"])
            tok[key, n] = do("pool", lambda e: e.tensor_scalar(
                dst, src, row[:, 8:9], row[:, 10:11], ALU.add, ALU.mult), a, *reuse)

        def ln1(m):
            i = m % NX
            reuse = () if m < 2 else (tok["t1", m - 2],) if m < 6 else (tok["xnl", m - 2],)
            norm(xs[:, i, :], xn[:, m % 2, :], st1, "xn", m, tok["load", m], reuse)

        def ln1_parts(m):
            hi, lo = xnhl[:, m % 4, 0, :], xnhl[:, m % 4, 1, :]
            reuse = (tok["xt", m - 4],) if m >= 8 else ()
            a = do("act", lambda e: e.activation(hi, xn[:, m % 2, :], ACT.Copy), tok["xn", m], *reuse)
            tok["xnl", m] = do("dve", lambda e: e.tensor_tensor(lo, xn[:, m % 2, :], hi, ALU.subtract), a, *reuse)

        def add_bp(m):
            i = m % NX
            tok["xb", m] = do("pool", lambda e: e.tensor_tensor(xs[:, i, :], xs[:, i, :], bp[:, :], ALU.add),
                              tok["xn", m], tok["bias"])

        def t1(m):
            j, t = divmod(m, 4)
            cols = slice(t * P, (t + 1) * P)
            if j:
                tok["xt", m] = q.dma("sp", lambda e: e.dma_start(
                    xt[:, :, cols], xnhl[:, t, :, :].rearrange("p a n -> p (a n)"), transpose=True),
                    f"xt{t}", 16 * j, tok["xnl", m], tok["qkv", j - 1, 8 + t])
                return
            r, free = take()
            tok["t1", m] = transposes(R[r], free, [xn[:, m % 2, k * P:(k + 1) * P] for k in range(4)],
                                      tok["xn", m], tok["ident"])
            tok["x32", m] = do("act", lambda e: e.activation(x32[:, :, cols], four(R[r][:, :]), ACT.Copy),
                               tok["t1", m])
            give(r, tok["x32", m])

        def t1_parts(m):
            cols = slice(m * P, (m + 1) * P)
            a = do("act", lambda e: e.activation(xth[:, :, cols], x32[:, :, cols], ACT.Copy), tok["x32", m])
            tok["xt", m] = do("pool", lambda e: e.tensor_tensor(xtl[:, :, cols], x32[:, :, cols], xth[:, :, cols],
                                                                ALU.subtract), a)

        def direct_q():
            banks = [(*take(), i) for i in range(3)]
            banks = [(R[r], r, free, i) for r, free, i in banks] + [(Y, None, (), 3)]
            for k in range(4):
                for bank, r, free, i in banks:
                    cols = slice(i * P, (i + 1) * P)
                    tok["qkv", 0, i] = group(r, free if k == 0 else (), [(bank[:, :], raw[:, k, cols], x32[:, k, :],
                                                                         k == 0, k == 3)],
                                             tok["wa", k], *(tok["x32", t] for t in range(4)))
            return banks

        def phi(j, i, bank, un):
            dst = qkv[j % 2]
            reuse = (tok["av", 4 * j - 5], tok["qc", j - 2, i % 4]) if j >= 2 else (tok["w", 1],) if j else ()
            do("act", lambda e: e.activation(dst[:, i, :], bank[:, :], ACT.Exp, scale=un, bias=bqk[:, i:i + 1]),
               tok["qkv", j, i], tok["bias"], *reuse)
            u = tok.get("nrel", 0)
            tok["nrel"] = u + 1
            a = do("act", lambda e: e.activation(rel[:, u % 2, :], bank[:, :], ACT.Relu, scale=un,
                                                 bias=bqk[:, i:i + 1]),
                   *((tok["phi_n", u - 2],) if u >= 2 else ()))
            tok["phi", j, i] = tok["phi_n", u] = do("dve", lambda e: e.scalar_tensor_tensor(
                dst[:, i, :], dst[:, i, :], 1.0, rel[:, u % 2, :], ALU.min, ALU.add), a)
            return a

        def proj_qkv(j, i):
            dst = qkv[j % 2]
            r, free = take()
            mms = []
            last_use = (tok["av", 4 * j - 5],) if j >= 2 else ()
            if i < 8:
                cols = slice(i * P, (i + 1) * P)
                for k in range(4):
                    for a, b in ((wh, xth), (wh, xtl), (wl, xth)):
                        mms.append((R[r][:, :], a[:, k, cols], b[:, k, :], not mms, len(mms) == 11))
                tok["qkv", j, i] = group(r, free, mms, *(tok["xt", 4 * j + t] for t in range(4)), tok["w", i // 2],
                                         tok["up_w"])
                give(r, phi(j, i, R[r], UN_W))
            else:
                t = i - 8
                cols = slice(t * P, (t + 1) * P)
                for k in range(4):
                    for a, b in ((xth, wh), (xth, wl), (xtl, wh)):
                        mms.append((R[r][:, :], a[:, k, cols], b[:, k, 2 * D:], not mms, len(mms) == 11))
                tok["qkv", j, i] = group(r, free, mms, tok["xt", 4 * j + t], tok["w", 5])
                tok["v", j, t] = do("dve", lambda e: e.scalar_tensor_tensor(
                    dst[:, i, :], R[r][:, :], UN_V, bv[:, :], ALU.mult, ALU.add),
                    tok["qkv", j, i], tok["up_w"], tok["bv"], *last_use)
                give(r, tok["v", j, t])

        def denominators(j, g):
            src = qkv[j % 2]
            u = 4 * j + g
            c = cum[:, g % 2, :]
            start = 0.0 if j % 2 == 0 else carry[:, g:g + 1]
            reuse = (tok["qcl", u - 2],) if u >= 2 else ()
            a = do("dve", lambda e: e.tensor_tensor_scan(c, src[:, 4 + g, :], src[:, 4 + g, :], start,
                                                         ALU.add, ALU.bypass),
                   tok["phi", j, 4 + g], *reuse, *((tok["carry", j - 1, g],) if j % 2 else ()))
            if j % 2 == 0:
                a = tok["carry", j, g] = do("dve", lambda e: e.tensor_copy(carry[:, g:g + 1], c[:, D - 1:D]), a)
            tok["qc", j, g] = do("pool", lambda e: e.tensor_tensor(c, c, src[:, g, :], ALU.mult), a,
                                 tok["phi", j, g])

        def den_parts(j, g):
            u = 4 * j + g
            c = cum[:, g % 2, :]
            reuse = (tok["den", u - 1],) if u else ()
            a = do("act", lambda e: e.activation(qch[:, :], c, ACT.Copy), tok["qc", j, g], *reuse)
            tok["qcl", u] = do("dve", lambda e: e.tensor_tensor(qcl[:, :], c, qch[:, :].bitcast(F32), ALU.subtract),
                               a, *reuse)

        def den(j, g):
            u = 4 * j + g
            r, free = take()
            mms = [(R[r][:, :], blkr[:, :], qch[:, :], True, False), (R[r][:, :], blkr[:, :], qcl[:, :], False, True)]
            tok["den", u] = group(r, free, mms, tok["blkr"], tok["qcl", u])
            reuse = (tok["y", 4 * j - 5],) if j >= 2 else (tok["wft"],)
            tok["dene", j, g] = do("act", lambda e: e.activation(rden[j % 2][:, g, :], R[r][:, :], ACT.Copy,
                                                                 bias=DEN_EPS), tok["den", u], *reuse)
            give(r, tok["dene", j, g])

        def invert(j, g, c):
            cols = slice(c * P, (c + 1) * P)
            tok["rden", j, g, c] = do("dve", lambda e: e.reciprocal(rden[j % 2][:, g, cols], rden[j % 2][:, g, cols]),
                                      tok["dene", j, g])

        def parts(n):
            j, c = divmod(n, 4)
            return qkv[j % 2], j, c, slice(c * P, (c + 1) * P)

        def k_tokens(n):
            src, j, c, cols = parts(n)
            if n % PER == PER - 1:
                return
            free = (tok["y", n - 2],) if n >= 2 else (tok["q_direct"],)
            a = transposes(Y, free, [src[:, 4 + g, cols] for g in range(4)],
                           *(tok["phi", j, 4 + g] for g in range(4)))
            tok["ktok", n] = do("act", lambda e: e.activation(ktok[:, n % 2, :], Y[:, :], ACT.Copy), a,
                                *((tok["delta", n - 2],) if ("delta", n - 2) in tok else ()))

        def scores(n, groups):
            src, j, c, cols = parts(n)
            mm = {}
            for g in groups:
                for h in range(4):
                    rows = slice(32 * h, 32 * h + 32)
                    free = (tok["s_read", n - 1, h],) if n and g == 0 else ()
                    mm[h] = do("pe", lambda e, g=g, h=h, rows=rows: e.matmul(
                        S[h][:, g * P:(g + 1) * P], src[rows, 4 + g, cols], src[rows, g, cols],
                        start=True, stop=True),
                        tok["phi", j, g], tok["phi", j, 4 + g], *free, tick=g == 3)
            if 3 not in groups:
                return
            for h in range(4):
                reuse = (tok["av", n - 1],) if n else (tok["xt", 3], tok["qkv", 0, 3])
                if h < (MASK_DVE if j + 1 < NB else 3):
                    tok["s_read", n, h] = tok["sm", n, h] = do("dve", lambda e, h=h: e.tensor_tensor(
                        four(sm[:, h, :]), four(S[h][:, :]), over(causal[:, :]), ALU.mult),
                        mm[h], tok["causal"], *reuse)
                else:
                    a = do("act", lambda e, h=h: e.activation(sm[:, h, :], S[h][:, :], ACT.Copy), mm[h], *reuse)
                    tok["s_read", n, h] = a
                    tok["sm", n, h] = do("pool", lambda e, h=h: e.affine_select(
                        out=four(sm[:, h, :]), in_=four(sm[:, h, :]), compare_op=ALU.is_ge, fill=0.0, base=0,
                        pattern=[[0, 4], [1, P]], channel_multiplier=-1), a)

        def update(n):
            src, j, c, cols = parts(n)
            if n % PER == PER - 1:
                return
            r, free = take()
            mms = [(R[r][32 * h:32 * h + 32, 32 * g:32 * g + 32], ktok[:, n % 2, at:at + 32], src[:, 8 + c, at:at + 32],
                    True, True) for g in range(4) for h in range(4) for at in [(4 * g + h) * 32]]
            tok["delta", n] = group(r, free, mms, tok["ktok", n], tok["v", j, c])
            waits = [tok["delta", n], tok["zeros"]]
            if n:
                waits.append(tok["av", n - 1])
            if n % PER:
                waits.append(tok["state", n])
            for h in range(4):
                rows = slice(32 * h, 32 * h + 32)
                fresh = R[r][rows, 0:P].rearrange("p (g m) -> p g m", g=4)
                new = four(state[rows, (n + 1) % 2, :])[:, :, rows]
                old = four(state[rows, n % 2, :])[:, :, rows]
                if n % PER == 0:
                    a = do("dve", lambda e, new=new, fresh=fresh: e.tensor_copy(new, fresh), *waits, tick=h == 3)
                else:
                    a = do("dve", lambda e, new=new, old=old, fresh=fresh: e.tensor_tensor(new, fresh, old, ALU.add),
                           *waits, tick=h == 3)
            tok["state", n + 1] = a
            give(r, a)

        def values(n):
            src, j, c, cols = parts(n)
            first = n % PER == 0
            free = [tok["y", n - 1]] if n else []
            if ("ktok", n + 1) in tok:
                free.append(tok["ktok", n + 1])
            if not first:
                for g in range(4):
                    do("pe", lambda e, g=g: e.matmul(
                        Y[:, g * P:(g + 1) * P], state[:, n % 2, g * P:(g + 1) * P], src[:, g, cols],
                        start=g == 0, stop=False, skip_group_check=True), tok["state", n], *free, tick=False)
            for g in range(4):
                for h in range(4):
                    col = (4 * g + h) * 32
                    a = do("pe", lambda e, g=g, h=h, col=col: e.matmul(
                        Y[32 * h:32 * h + 32, g * P:(g + 1) * P], src[:, 8 + c, col:col + 32],
                        sm[:, h, g * P:(g + 1) * P], start=first and g == 0, stop=True, skip_group_check=True),
                        tok["sm", n, h], tok["v", j, c], *free, tick=g == 3 and h == 3)
            tok["av", n] = a
            reuse = (tok["yl", n - 1], tok["yh", n - 1]) if n else ()
            tok["y", n] = do("dve", lambda e: e.tensor_tensor(four(y[:, :]), four(Y[:, :]),
                                                                  rden[j % 2][:, :, cols], ALU.mult),
                             a, *(tok["rden", j, g, c] for g in range(4)), *reuse)
            reuse = (tok["proj", n - 2],) if n >= 2 else ()
            tok["yh", n] = do("act", lambda e: e.activation(yh[:, n % 2, :], y[:, :], ACT.Copy), tok["y", n], *reuse)
            tok["yl", n] = do("pool", lambda e: e.tensor_tensor(
                yl[:, n % 2, :], y[:, :], yh[:, n % 2, :], ALU.subtract), tok["yh", n], *reuse)

        def proj(n):
            r, free = take()
            pairs = [(yh, b, g) for b in (wph, wpl) for g in range(4)] + [(yl, wph, g) for g in range(4)]
            mms = [(R[r][:, :], a[:, n % 2, g * P:(g + 1) * P], b[:, g, :], i == 0, i == 11)
                   for i, (a, b, g) in enumerate(pairs)]
            group(r, free, mms[:8], tok["yh", n], tok["wpl"])
            tok["proj", n] = group(r, (), mms[8:], tok["yl", n])
            x = xs[:, n % NX, :]
            a = do("dve", lambda e: e.scalar_tensor_tensor(x, R[r][:, :], UN_P, x, ALU.mult, ALU.add),
                   tok["proj", n], tok["xb", n])
            give(r, a)
            norm(x, x2[:, n % 2, :], st2, "x2", n, a, (tok["x28", n - 2] if n >= 2 else tok["wf_tmp"],))
            tok["x1b", n] = do("pool", lambda e: e.tensor_tensor(x, x, bf[:, :], ALU.add), tok["x2", n])

        def t2(n):
            i = n % 2
            if n >= NT - 2:
                r, free = take()
                a = transposes(R[r], free, [x2[:, i, k * P:(k + 1) * P] for k in range(4)], tok["x2", n])
                a = tok["x28", n] = do("act", lambda e: e.activation(x28[:, :], R[r][:, :], ACT.Copy, saturate=False),
                                       a, tok["x2b", n - 1])
                give(r, a)
                tok["x2t", n] = tok["x2b", n] = do("act", lambda e: e.activation(
                    x2t[:, i, :, :], four(x28[:, :]), ACT.Copy), a, tok["ffn", n - 2])
                return
            a = tok["x28", n] = do("act", lambda e: e.activation(x28[:, :], x2[:, i, :], ACT.Copy, saturate=False),
                                   tok["x2", n], *((tok["x2b", n - 1],) if n else ()))
            tok["x2b", n] = do("act", lambda e: e.activation(x2b[:, i, :], x28[:, :], ACT.Copy), a,
                               *((tok["x2t", n - 2],) if n >= 2 else ()))
            tok["x2t", n] = q.dma("sp", lambda e: e.dma_start(x2t[:, i, :, :], x2b[:, i, :], transpose=True),
                                  f"x2t{i}", 16 * (n // 2 + 1), tok["x2b", n],
                                  *((tok["ffn", n - 2],) if n >= 2 else ()))

        def ffn(n):
            r, free = take()
            mms = [(R[r][:, :], x2t[:, n % 2, k, :], wft[:, k, :], k == 0, k == 3) for k in range(4)]
            tok["ffn", n] = group(r, free, mms, tok["x2t", n], tok["wft"])
            a = do("act", lambda e: e.activation(o16[:, n % 2, :], R[r][:, :], ACT.Copy), tok["ffn", n],
                   *((tok["out", n - 2],) if n >= 2 else ()))
            give(r, a)
            x = xs[:, n % NX, :]
            tok["out", n] = do("dve", lambda e: e.tensor_tensor(x, o16[:, n % 2, :], x, ALU.add), a, tok["x1b", n])
            tok["store", n] = q.dma("sp", lambda e: e.dma_start(out_d[n * P:(n + 1) * P, :], x),
                                    f"xo{n % NX}", 16 * (n // NX + 1), tok["out", n])

        def pow2(dst, src, *waits):
            return do("dve", lambda e: e.tensor_scalar(dst.bitcast(I32), src.bitcast(I32), 0x7F800000, None,
                                                       ALU.bitwise_and), *waits)

        def peak(src, dst, *waits):
            return do("dve", lambda e: e.tensor_reduce(dst, src, AX.X, ALU.max, apply_absolute_value=True), *waits)

        def scale(at, top, free):
            a = do("pool", lambda e: e.partition_all_reduce(wm[:, at + 1:at + 2], wm[:, at:at + 1], P,
                                                            bass.bass_isa.ReduceOp.absmax), top, free)
            tok["pool_ready"] = do("pool", lambda e: e.memset(wm[:, at + 6:at + 7], 0.0), a)
            a = do("dve", lambda e: e.tensor_scalar(wm[:, at + 2:at + 3], wm[:, at + 1:at + 2], 2.0 ** -80, 2.0 ** 80,
                                                    ALU.max, ALU.min), a)
            a = pow2(wm[:, at + 3:at + 4], wm[:, at + 2:at + 3], a)
            a = do("dve", lambda e: e.tensor_scalar(wm[:, at + 4:at + 5], wm[:, at + 3:at + 4], 2.0 ** -13, None,
                                                    ALU.mult), a)
            return do("dve", lambda e: e.reciprocal(wm[:, at + 5:at + 6], wm[:, at + 4:at + 5]), a)

        ln1(0)
        for m in range(4):
            if m < 3:
                ln1(m + 1)
            t1(m)
        banks = direct_q()
        for k in range(4):
            a = peak(raw[:, k, :], wm[:, 20 + k:21 + k], tok["wa", k])
            if k > 0:
                t1_parts(k - 1)
        a = peak(wm[:, 20:24], wm[:, 0:1], a)
        tok["up_w"] = scale(0, a, tok["blk"])
        t1_parts(3)

        def attn_weight(i):
            cols = slice(i * 256, (i + 1) * 256)
            a = do("act", lambda e: e.activation(wh[:, :, cols], raw[:, :, cols], ACT.Copy, scale=UP_W),
                   tok["up_w"])
            tok["w", i] = do("dve", lambda e: e.scalar_tensor_tensor(
                wl[:, :, cols], raw[:, :, cols], UP_W, wh[:, :, cols], ALU.mult, ALU.subtract), a)

        def v_scale():
            a = peak(bv[:, :], wm[:, 14:15], tok["bias"], tok["up_w"])
            a = do("dve", lambda e: e.scalar_tensor_tensor(wm[:, 15:16], wm[:, 3:4], 2.0 * D, wm[:, 14:15],
                                                           ALU.mult, ALU.add), a)
            a = pow2(wm[:, 16:17], wm[:, 15:16], a)
            a = do("dve", lambda e: e.tensor_scalar(wm[:, 17:18], wm[:, 16:17], 2.0 ** -14, None, ALU.mult), a)
            a = do("dve", lambda e: e.reciprocal(wm[:, 18:19], wm[:, 17:18]), a)
            do("dve", lambda e: e.tensor_tensor(wm[:, 19:20], wm[:, 4:5], wm[:, 18:19], ALU.mult), a, tick=False)
            tok["bv"] = do("dve", lambda e: e.tensor_scalar(bv[:, :], bv[:, :], wm[:, 18:19], None, ALU.mult))

        def proj_scale():
            a = peak(raw_p.rearrange("p k n -> p (k n)"), wm[:, 7:8], tok["wp"])
            a = tok["up_p"] = scale(7, a, tok["pool_ready"])
            do("dve", lambda e: e.tensor_tensor(wm[:, 24:25], wm[:, 11:12], wm[:, 17:18], ALU.mult), a, tick=False)

        def proj_weight():
            a = do("act", lambda e: e.activation(wph[:, :, :], raw_p, ACT.Copy, scale=UP_P), tok["up_p"])
            tok["wpl"] = do("dve", lambda e: e.scalar_tensor_tensor(wpl[:, :, :], raw_p, UP_P, wph[:, :, :],
                                                                    ALU.mult, ALU.subtract), a)

        def ffn_weight():
            w = rden[1][:, :, :]
            lo = x2[:, 0, :].bitcast(F8).rearrange("p (k n) -> p k n", k=4)
            hi = x2[:, 1, :].bitcast(F8).rearrange("p (k n) -> p k n", k=4)
            tmp = rden[0][:, :, :]
            a = do("dve", lambda e: e.tensor_scalar(lo, w, 240.0, -240.0, ALU.min, ALU.max, saturate=False),
                   tok["wf"])
            yield
            a = do("dve", lambda e: e.tensor_scalar(tmp, w, 0.5, 224.0, ALU.mult, ALU.min))
            a = do("dve", lambda e: e.tensor_scalar(hi, tmp, -224.0, None, ALU.max, saturate=False), a)
            yield
            b = do("pool", lambda e: e.tensor_tensor(w, w, w, ALU.mult), a)
            yield
            a = do("dve", lambda e: e.scalar_tensor_tensor(tmp, hi, 2.0, lo, ALU.mult, ALU.subtract), a)
            yield
            b = do("dve", lambda e: e.tensor_scalar(w, w, 128.0 * 128.0, None, ALU.is_gt), b)
            a = do("pool", lambda e: e.tensor_tensor(tmp, tmp, w, ALU.mult), a, b)
            yield
            a = do("pool", lambda e: e.tensor_tensor(w, tmp, lo, ALU.add), a)
            tok["wf_tmp"] = a
            yield
            for k in range(4):
                r, free = take()
                b = transposes(R[r], free, [w[:, f, k * P:(k + 1) * P] for f in range(4)], a, tok["ident"])
                tok["wft"] = do("act", lambda e, r=r, k=k: e.activation(wft[:, k, :], R[r][:, :], ACT.Copy), b)
                give(r, tok["wft"])
            yield

        weight = ffn_weight()
        def direct_phi(i):
            bank, r, _, _ = banks[i]
            a = tok["q_direct"] = phi(0, i, bank, 1.0)
            if r is not None:
                give(r, a)

        attn_weight(2)
        next(weight)
        next(weight)
        next(weight)
        direct_phi(0)
        attn_weight(3)
        direct_phi(1)
        direct_phi(2)
        next(weight)
        proj_qkv(0, 4)
        direct_phi(3)
        ln1(4)
        attn_weight(4)
        proj_qkv(0, 5)
        ln1(5)
        next(weight)
        attn_weight(5)
        proj_qkv(0, 6)
        v_scale()
        ln1_parts(4)
        ln1_parts(5)
        ln1(6)
        proj_qkv(0, 7)
        ln1(7)
        next(weight)
        attn_weight(0)
        for t in range(4):
            proj_qkv(0, 8 + t)
            if t == 0:
                ln1_parts(6)
                ln1_parts(7)
            if t == 1:
                attn_weight(1)
            t1(4 + t)
        next(weight)
        k_tokens(0)
        denominators(0, 0)
        denominators(0, 1)
        proj_scale()

        order = (0, 4, 1, 5, 2, 6, 3, 7, 8, 9, 10, 11)
        follow = {i: [] for i in range(14)}
        for g in range(4):
            i = 2 * g + 2
            follow[i + 3].append((den, g))
            for c in range(4):
                follow[i + 4 + c // 2].append((invert, g, c))
            follow[i].append((denominators, g))
            follow[i + 1].append((den_parts, g))

        def ahead_of(j, i):
            if j < NB:
                proj_qkv(j, order[i])
                run(follow[i], j)

        def run(steps, j):
            for fn, *args in steps:
                fn(j, *args)

        first = ([(den_parts, 0)],
                 [(den, 0), (denominators, 2), (den_parts, 1)],
                 [(den, 1), (denominators, 3), (den_parts, 2)],
                 [(den, 2), (den_parts, 3)],
                 [(den, 3)] + [(invert, g, 0) for g in range(4)])
        for n in range(NT + 2):
            j, c = divmod(n, 4)
            if n < NT:
                last = c == 3 and j + 2 < NB
                if n + 8 < NT:
                    ln1(n + 8)
                    add_bp(n + 8)
                now = first if n == 0 else ((),) * 5
                scores(n, (0, 1))
                run(now[0], 0)
                if c == 0 and j:
                    run(follow[12], j)
                if last:
                    t1(4 * j + 8)
                ahead_of(j + 1, 3 * c)
                if c == 0 and j:
                    run(follow[13], j)
                run(now[1], 0)
                if j == 0 and c:
                    for g in range(2):
                        invert(0, g, c)
                scores(n, (2, 3))
                if j + 1 == NB:
                    proj(n - 1)
                run(now[2], 0)
                if n + 8 < NT:
                    ln1_parts(n + 8)
                if n == 0:
                    proj_weight()
                    for m in range(8):
                        add_bp(m)
                if last:
                    t1(4 * j + 9)
                ahead_of(j + 1, 3 * c + 1)
                run(now[3], 0)
            if n == NT:
                proj(NT - 1)
            if 2 <= n:
                t2(n - 2)
            if n < NT:
                if last:
                    t1(4 * j + 10)
                update(n)
                if n + 1 < NT:
                    k_tokens(n + 1)
                if j == 0 and c:
                    for g in range(2, 4):
                        invert(0, g, c)
                ahead_of(j + 1, 3 * c + 2)
                if last:
                    t1(4 * j + 11)
                if n + 10 < NT:
                    load_x(n + 10)
                run(now[4], 0)
                values(n)
            if 1 <= n < NT and j + 1 < NB:
                proj(n - 1)
            if 2 <= n:
                ffn(n - 2)
        q.ops["sp"].append(([tok["store", n] for n in range(NT - NX, NT)], None, None))

        block = ctx.enter_context(nc.Block())

        @block.sync
        def _(e):
            last = q.ops["sp"].pop()
            q.run("sp", e, sems)
            for name, value in last[0]:
                e.wait_ge(sems[name], value)

        @block.scalar
        def _(e):
            q.run("act", e, sems)

        @block.vector
        def _(e):
            q.run("dve", e, sems)

        @block.gpsimd
        def _(e):
            q.run("pool", e, sems)

        @block.tensor
        def _(e):
            q.run("pe", e, sems)


_INS = ["L0_attn_x", "L0_attn_W_attn", "L0_attn_b_attn", "L0_attn_W_proj", "L0_attn_b_proj", "L0_ffn_weight",
        "L0_ffn_bias"]


def kernel(**inputs):
    import numpy as np
    import concourse.bacc as bacc
    from concourse.bass_utils import run_bass_kernel_spmd

    nc = bacc.Bacc("TRN2", target_bir_lowering=False, num_devices=1)
    arrays, args = {}, []
    for name in _INS:
        a = np.ascontiguousarray(inputs[name])
        if name == "L0_attn_x":
            a = a.reshape(B * T, D)
        arrays[f"in_{name}"] = a
        args.append(nc.dram_tensor(f"in_{name}", a.shape, mybir.dt.from_np(a.dtype), kind="ExternalInput").ap())
    args.append(nc.dram_tensor("out_0", (B * T, D), F32, kind="ExternalOutput").ap())
    build(nc, *args)
    r = run_bass_kernel_spmd(nc, [arrays], core_ids=[0])
    return r.results[0]["out_0"].reshape(B, T, D)
```
